# Optimizing a Trainium2 kernel written in Bass

```python
import numpy as np
import jax
import jax.numpy as jnp

def _softmax(x, axis=-1):
    return jax.nn.softmax(x, axis=axis)

def _gelu(x):
    return jax.nn.gelu(x, approximate=True)

def _silu(x):
    return jax.nn.silu(x)

def _sigmoid(x):
    return jax.nn.sigmoid(x)

def _layernorm(x, axis=-1, eps=1e-05):
    m = jnp.mean(x, axis=axis, keepdims=True)
    v = jnp.var(x, axis=axis, keepdims=True)
    return (x - m) / jnp.sqrt(v + eps)

def _scatter_add(tgt, idx, src, axis=0):
    return tgt.at[idx].add(src)

def _segment_sum(src, seg, n):
    return jax.ops.segment_sum(src, seg, n)
kernel_name = 'mk_macaron_d1_jaxref_r8_a8f6b9'

def setup_inputs(seed: int=0):
    np.random.seed(seed)
    _w = jnp.asarray

    def _L0_attn_setup():
        import jax, jax.numpy as jnp
        import numpy as np
        B, L = (2, 512)
        D_MODEL, D_INNER, D_STATE, D_CONV, DT_RANK = (128, 256, 16, 4, 64)
        EPS = 1e-05
        key = jax.random.key(seed)
        ks = jax.random.split(key, 8)
        s = lambda k, shape, scale=0.02: jax.random.normal(k, shape, jnp.float32) * scale
        A_init = jnp.tile(jnp.arange(1, D_STATE + 1, dtype=jnp.float32), (D_INNER, 1))
        return {'x': jax.random.normal(ks[0], (B, L, D_MODEL), jnp.float32), 'W_in': s(ks[1], (D_MODEL, 2 * D_INNER)), 'conv_w': s(ks[2], (D_INNER, D_CONV), 0.2), 'conv_b': jnp.zeros((D_INNER,), jnp.float32), 'W_x': s(ks[3], (D_INNER, DT_RANK + 2 * D_STATE)), 'W_dt': s(ks[4], (DT_RANK, D_INNER), 0.1), 'b_dt': jnp.full((D_INNER,), -4.6, jnp.float32), 'A_log': jnp.log(A_init), 'D_skip': jnp.ones((D_INNER,), jnp.float32), 'W_out': s(ks[5], (D_INNER, D_MODEL)), 'ln_g': jnp.ones((D_MODEL,), jnp.float32), 'ln_b': jnp.zeros((D_MODEL,), jnp.float32)}
    _L0_attn_in = _L0_attn_setup()

    def _L0_ffn_setup():
        import jax, jax.numpy as jnp
        import numpy as np
        B, S, DIM, FFN, E = (4, 256, 128, 512, 8)
        key = jax.random.key(seed)
        k0, k1, k2, k3 = jax.random.split(key, 4)
        scale = 0.02
        return {'hidden_states': jax.random.normal(k0, (B, S, DIM), jnp.float32), 'router_w': jax.random.normal(k1, (DIM, E), jnp.float32) * scale, 'router_b': jnp.zeros((E,), jnp.float32), 'w1': jax.random.normal(k2, (E, DIM, 2 * FFN), jnp.float32) * scale, 'w2': jax.random.normal(k3, (E, FFN, DIM), jnp.float32) * scale}
    _L0_ffn_in = _L0_ffn_setup()
    _d = {'L0_attn_x': _L0_attn_in['x'], 'L0_attn_W_in': _L0_attn_in['W_in'], 'L0_attn_conv_w': _L0_attn_in['conv_w'], 'L0_attn_conv_b': _L0_attn_in['conv_b'], 'L0_attn_W_x': _L0_attn_in['W_x'], 'L0_attn_W_dt': _L0_attn_in['W_dt'], 'L0_attn_b_dt': _L0_attn_in['b_dt'], 'L0_attn_A_log': _L0_attn_in['A_log'], 'L0_attn_D_skip': _L0_attn_in['D_skip'], 'L0_attn_W_out': _L0_attn_in['W_out'], 'L0_attn_ln_g': _L0_attn_in['ln_g'], 'L0_attn_ln_b': _L0_attn_in['ln_b'], 'L0_ffn_router_w': _L0_ffn_in['router_w'], 'L0_ffn_router_b': _L0_ffn_in['router_b'], 'L0_ffn_w1': _L0_ffn_in['w1'], 'L0_ffn_w2': _L0_ffn_in['w2']}
    _x0 = _d['L0_attn_x']
    _d['L0_attn_x'] = jax.random.normal(jax.random.fold_in(jax.random.key(seed), 1), (2, 1024, 128), dtype=_x0.dtype)
    del _x0
    return _d

def reference(L0_attn_x, L0_attn_W_in, L0_attn_conv_w, L0_attn_conv_b, L0_attn_W_x, L0_attn_W_dt, L0_attn_b_dt, L0_attn_A_log, L0_attn_D_skip, L0_attn_W_out, L0_attn_ln_g, L0_attn_ln_b, L0_ffn_router_w, L0_ffn_router_b, L0_ffn_w1, L0_ffn_w2):

    def _L0_attn_ref(x, W_in, conv_w, conv_b, W_x, W_dt, b_dt, A_log, D_skip, W_out, ln_g, ln_b):
        import jax, jax.numpy as jnp
        import numpy as np
        B, L = (2, 512)
        D_MODEL, D_INNER, D_STATE, D_CONV, DT_RANK = (128, 256, 16, 4, 64)
        EPS = 1e-05
        Bsz, Lseq, _ = x.shape
        xz = x @ W_in
        xc, z = jnp.split(xz, 2, axis=-1)
        xp = jnp.pad(xc, ((0, 0), (D_CONV - 1, 0), (0, 0)))
        xc = sum((xp[:, k:k + Lseq, :] * conv_w[:, k] for k in range(D_CONV))) + conv_b
        xc = jax.nn.silu(xc)
        dbl = xc @ W_x
        dt_r = dbl[..., :DT_RANK]
        Bm = dbl[..., DT_RANK:DT_RANK + D_STATE]
        Cm = dbl[..., DT_RANK + D_STATE:]
        dt = jax.nn.softplus(dt_r @ W_dt + b_dt)
        A = -jnp.exp(A_log)

        def step(h, inps):
            x_t, dt_t, B_t, C_t = inps
            dA = jnp.exp(dt_t[..., None] * A)
            h = dA * h + (dt_t * x_t)[..., None] * B_t[:, None, :]
            y_t = jnp.einsum('bds,bs->bd', h, C_t)
            return (h, y_t)
        h0 = jnp.zeros((Bsz, D_INNER, D_STATE), x.dtype)
        xs = (xc.transpose(1, 0, 2), dt.transpose(1, 0, 2), Bm.transpose(1, 0, 2), Cm.transpose(1, 0, 2))
        _, ys = jax.lax.scan(step, h0, xs)
        y = ys.transpose(1, 0, 2) + xc * D_skip
        y = y * jax.nn.silu(z)
        out = y @ W_out
        mu = out.mean(-1, keepdims=True)
        var = out.var(-1, keepdims=True)
        return (out - mu) / jnp.sqrt(var + EPS) * ln_g + ln_b

    def _L0_ffn_ref(hidden_states, router_w, router_b, w1, w2):
        import jax, jax.numpy as jnp
        import numpy as np
        B, S, DIM, FFN, E = (4, 256, 128, 512, 8)
        b, s, d = hidden_states.shape
        x = hidden_states.reshape(-1, d)
        logits = x @ router_w + router_b
        route = jax.nn.softmax(logits, axis=1)
        max_prob = jnp.max(route, axis=1, keepdims=True)
        max_ind = jnp.argmax(route, axis=1)
        out = jnp.zeros_like(x)
        num_experts = w1.shape[0]
        for e in range(num_experts):
            h = x @ w1[e]
            a, g = jnp.split(h, 2, axis=1)
            y = jax.nn.silu(a) * g @ w2[e]
            out = jnp.where((max_ind == e)[:, None], y, out)
        out = out * max_prob
        return out.reshape(b, s, d)
    x = L0_attn_x
    x = x + 0.5 * _L0_ffn_ref(_layernorm(x, axis=-1), L0_ffn_router_w, L0_ffn_router_b, L0_ffn_w1, L0_ffn_w2)
    x = x + _L0_attn_ref(_layernorm(x, axis=-1), L0_attn_W_in, L0_attn_conv_w, L0_attn_conv_b, L0_attn_W_x, L0_attn_W_dt, L0_attn_b_dt, L0_attn_A_log, L0_attn_D_skip, L0_attn_W_out, L0_attn_ln_g, L0_attn_ln_b)
    x = x + 0.5 * _L0_ffn_ref(_layernorm(x, axis=-1), L0_ffn_router_w, L0_ffn_router_b, L0_ffn_w1, L0_ffn_w2)
    return x

_drawn_inputs = setup_inputs


def setup_inputs(seed=0):
    import zlib

    import numpy as np

    out = dict(_drawn_inputs(seed))
    spreads = {'L0_attn_conv_b': (0.0, 0.1),
     'L0_attn_b_dt': (-4.599999904632568, 0.6),
     'L0_attn_D_skip': (1.0, 0.2),
     'L0_attn_ln_g': (1.0, 0.2),
     'L0_attn_ln_b': (0.0, 0.1),
     'L0_ffn_router_b': (0.0, 0.8)}
    factors = {'L0_attn_W_x': 8.0,
     'L0_attn_W_dt': 8.0,
     'L0_attn_A_log': 8.0,
     'L0_ffn_router_w': 8.0,
     'L0_ffn_w1': 8.0,
     'L0_ffn_w2': 8.0}
    for name, (base, spread) in spreads.items():
        noise = np.random.default_rng([zlib.crc32(name.encode()), seed]).standard_normal(out[name].shape)
        drawn = base * np.exp(spread * noise) if base else spread * noise
        out[name] = jnp.asarray(drawn.astype(out[name].dtype))
    for name, factor in factors.items():
        out[name] = (out[name] * factor).astype(out[name].dtype)
    return out
```

```python
from contextlib import ExitStack

import concourse.bass as bass
from concourse import mybir

ALU = mybir.AluOpType
ACT = mybir.ActivationFunctionType
AX = mybir.AxisListType
F32 = mybir.dt.float32
BF16 = mybir.dt.bfloat16
I32 = mybir.dt.int32
U32 = mybir.dt.uint32

P = 128
EPS = 1e-5


GROUP = 4


def macaron_kernel(nc, x_in, W_in, conv_w, conv_b, W_x, W_dt, b_dt, A_log, D_skip, W_out, ln_g, ln_b,
                   router_w, router_b, w1, w2, out):
    B, L, D = x_in.shape
    N = B * L
    NT = N // P
    NG = NT // GROUP
    E = router_w.shape[1]
    F = w2.shape[1]
    FC = F // P
    DI = W_out.shape[0]
    NH = DI // P
    S = A_log.shape[1]
    TAPS = conv_w.shape[1]
    R = W_dt.shape[0]
    CH = 512
    NC = N // CH
    CPB = L // CH
    SLOT_TILES = (N + E * (P - 1)) // P
    PAD = TAPS - 1
    LOG_P = P.bit_length() - 1
    M_LOADS = 12 + 2 * NH
    ds = bass.ds
    assert D == P and NH == 2 and E == 8 and 2 * S == 32 and SLOT_TILES % 2 == 1

    with ExitStack() as ctx:
        def sb(name, shape, dt=F32):
            return ctx.enter_context(nc.sbuf_tensor(name, shape, dt))

        def sem(name):
            return ctx.enter_context(nc.semaphore(name))

        xn_rows = nc.dram_tensor("xn_rows", (N, D), F32).ap()
        y_rows = nc.dram_tensor("y_rows", (N + SLOT_TILES * P, D), F32).ap()

        ident = sb("ident", [P, P])
        earlier = sb("earlier", [P, P], BF16)
        ones = sb("ones", [P, P], BF16)
        expert_iota_i = sb("expert_iota_i", [P, NT, E], I32)
        expert_iota = sb("expert_iota", [P, NT, E])
        tile_iota_i = sb("tile_iota_i", [P, SLOT_TILES], I32)
        tile_iota = sb("tile_iota", [P, SLOT_TILES])
        lane_iota = sb("lane_iota", [P, P], I32)
        token_tile_i = sb("token_tile_i", [P, NT], I32)
        token_tile = sb("token_tile", [P, NT])
        partition_i = sb("partition_i", [P, 1], I32)
        partition = sb("partition", [P, 1])
        spare_row_i = sb("spare_row_i", [P, SLOT_TILES], I32)
        spare_row = sb("spare_row", [P, SLOT_TILES])
        scan_keep = sb("scan_keep", [P, E, NT])
        ones_e = sb("ones_e", [P, E])
        pick_row = sb("pick_row", [3 * 2 * S, 2 * S], BF16)

        w1_sb = sb("w1_sb", [P, E * 2 * F])
        w2_sb = sb("w2_sb", [P, E * FC * D])
        router_sb = sb("router_sb", [P, E])
        router_b_sb = sb("router_b_sb", [P, E])
        W_in_sb = sb("W_in_sb", [P, 2 * DI])
        W_dtr_sb = sb("W_dtr_sb", [P, NH, R])
        W_bc_sb = sb("W_bc_sb", [P, NH, 3, 2 * S])
        W_dt_sb = sb("W_dt_sb", [R + 1, DI])
        W_out_sb = sb("W_out_sb", [P, NH, D])
        conv_w_sb = sb("conv_w_sb", [P, NH, TAPS])
        conv_b_sb = sb("conv_b_sb", [P, NH])
        D_skip_sb = sb("D_skip_sb", [P, NH])
        D_diag = sb("D_diag", [P, NH, P])
        A_sb = sb("A_sb", [P, NH, S])
        neg_A = sb("neg_A", [P, NH * S])
        ln_g_sb = sb("ln_g_sb", [P, D])
        ln_b_sb = sb("ln_b_sb", [P, D])

        x_tok = sb("x_tok", [P, NT * D])
        xn_tok = sb("xn_tok", [P, NT * D])
        xnT = sb("xnT", [P, N])
        y_tok = xnT

        stats = sb("stats", [P, NT, 6])
        mean = sb("mean", [P, NT])
        mean_diff = sb("mean_diff", [P, NT])
        var = sb("var", [P, NT])
        std = sb("std", [P, NT])
        rstd_try = sb("rstd_try", [P, NT])
        rstd_fix = sb("rstd_fix", [P, NT])
        rstd = sb("rstd", [P, NT])
        shift = sb("shift", [P, NT])

        logits = sb("logits", [P, NT, E])
        top_logit = sb("top_logit", [P, NT])
        expo = sb("expo", [P, NT, E])
        expo_sum = sb("expo_sum", [P, NT])
        half_prob = sb("half_prob", [P, NT])
        below_top = sb("below_top", [P, NT, E])
        first_top = sb("first_top", [P, NT])
        chosen = sb("chosen", [P, E, NT], BF16)
        upto_tile = sb("upto_tile", [P, E * NT])
        expert_tiles_i = sb("expert_tiles_i", [P, E], I32)
        expert_tiles = sb("expert_tiles", [P, E])
        last_tile = sb("last_tile", [P, E])
        first_tile = sb("first_tile", [P, E])
        slot_of = sb("slot_of", [P, E, NT])
        slot_f = sb("slot_f", [P, NT])
        slot = sb("slot", [P, NT], I32)
        slot_tile = sb("slot_tile", [P, NT], I32)
        slot_lane = sb("slot_lane", [P, NT], I32)
        slot_info = sb("slot_info", [P, 3, SLOT_TILES])
        slot_token = sb("slot_token", [P, SLOT_TILES])
        spare = sb("spare", [P, SLOT_TILES])
        gather_row = sb("gather_row", [P, SLOT_TILES], U32)
        scatter_row = sb("scatter_row", [P, SLOT_TILES], U32)
        tile_past = sb("tile_past", [1, SLOT_TILES, E])
        tile_expert_f = sb("tile_expert_f", [1, SLOT_TILES])
        tile_expert = sb("tile_expert", [1, SLOT_TILES], I32)

        phase = sb("phase", [P, NH * B * (PAD + L) + 16 * CH])

        def carve(*shapes):
            views, at = [], 0
            for rows, *dims in shapes:
                size = 1
                for n in dims:
                    size *= n
                flat = phase[0:rows, at:at + size]
                names = "abc"[:len(dims)]
                if len(dims) > 1:
                    flat = flat.rearrange(f"p ({' '.join(names)}) -> p {' '.join(names)}", **dict(zip(names, dims)))
                views.append(flat)
                at += size
            assert at <= phase.shape[1]
            return views

        xs_sb, xsT_sb, gate_sb, u_sb, uT_sb, ys_sb, lanes, tiles3 = carve(
            (P, 2, D), (P, 2, P), (P, 2, F), (P, 2, F), (P, 2, F), (P, 2, D), (P, NT * P // 2),
            (P, NT * 3 * SLOT_TILES // 2))
        at_lane = lanes.bitcast(BF16).rearrange("p (j m) -> p j m", m=P)
        at_tile = tiles3.bitcast(BF16).rearrange("p (j a t) -> p j a t", a=3, t=SLOT_TILES)
        xc_pre, dt_rank, soft_exp, soft_ln, soft_err, bc_rest = carve(
            (P, NH, B, PAD + L), (R + 1, 2, CH), (P, 2, NH, CH), (P, 2, NH, CH), (P, 2, NH, CH), (64, 2, CH))
        H, B_sb, dBx, hC, y_sb, yz = carve(
            (P, 2, NH, CH), (P, 2, CH), (P, 2, NH, CH), (P, 2, NH, CH), (P, NH, CH), (P, NH, CH))

        xc = sb("xc", [P, NH, N])
        silu_z = sb("silu_z", [P, NH, N])
        dt = sb("dt", [P, NH, N])
        dtx = sb("dtx", [P, NH, N])
        carry = sb("carry", [P, S * NH])
        bc_parts = sb("bc_parts", [96, N + CH], BF16)

        psum = ctx.enter_context(nc.psum_tensor("psum", [P, 8, 512], F32))

        loaded_x = sem("loaded_x")
        loaded_small = sem("loaded_small")
        loaded_w = sem("loaded_w")
        loaded_m = sem("loaded_m")
        consts_ready = sem("consts_ready")
        pool_step = sem("pool_step")
        dve_step = sem("dve_step")
        out_stored = sem("out_stored")
        pool_count, dve_count = [0], [0]

        def norm_sems(tag):
            return {n: sem(f"{tag}_{n}") for n in (
                "stats_done", "var_ready", "std_ready", "shift_ready", "xn_even", "xn_odd", "xnT_psum", "xnT_ready")}

        def ffn_sems(tag):
            f = {n: sem(f"{tag}_{n}") for n in (
                "logits_psum", "sub_ready", "expo_ready", "chosen_ready", "prefix_psum", "at_tile_ready",
                "at_lane_ready", "info_psum", "gather_row_ready", "scatter_row_ready", "tile_expert_ready", "xn_stored",
                "xsT_psum", "xsT_ready", "h_a", "h_g", "gate_ready", "u_ready", "uT_psum", "uT_ready", "ys_psum",
                "ys_ready", "combined")}
            f["y_loaded"] = [sem(f"{tag}_y_loaded{g}") for g in range(NG)]
            f["xs_loaded"] = [sem(f"{tag}_xs_loaded{k}") for k in range(2)]
            f["ys_stored"] = [sem(f"{tag}_ys_stored{k}") for k in range(2)]
            f["norm"] = norm_sems(tag)
            return f

        FF = [ffn_sems("ffn0"), ffn_sems("ffn1")]
        M = {n: sem(f"m_{n}") for n in (
            "A_exp", "neg_A_ready", "pads_clear", "xc_psum", "z_psum", "xc_pre_ready", "silu_z_ready", "conv_step",
            "xc_ready", "proj_psum", "dtr_ready", "v_psum", "soft_abs_ready", "soft_exp_ready", "soft_ln_ready",
            "round_ready", "err_ready", "lnerr_ready", "dt_ready", "dtx_ready", "bc1_ready", "bc_rest_ready",
            "bc2_ready", "bc3_ready", "x_plus_b", "B_psum", "B_ready", "C_psum", "dA_ready", "dBx_ready", "scan_done",
            "hC_ready", "sum_done", "carry_clear", "carry_ready", "y_ready", "yz_ready", "o_psum", "o_ready",
            "scale_ready", "x_ready", "scale_ready_pool", "x_ready_pool")}
        M["norm"] = norm_sems("m")
        M["out_norm"] = norm_sems("mo")

        def norm_statistics(dve, s, src, arrives):
            for j in range(NT):
                if arrives and j % GROUP == 0:
                    signal, by_group = arrives
                    dve.wait_ge(signal, by_group * (j // GROUP + 1))
                last = nc.vector.bn_stats(stats[:, j, :], src[:, j * D:(j + 1) * D])
            last.then_inc(s["stats_done"], 1)
            dve.wait_ge(s["stats_done"], 1)
            mean_even, mean_odd = stats[:, :, 1], stats[:, :, 4]
            nc.vector.tensor_tensor(mean_diff[:], mean_even, mean_odd, ALU.subtract)
            nc.vector.tensor_tensor(mean[:], mean_even, mean_odd, ALU.add)
            chain(dve, nc.vector.tensor_tensor(var[:], stats[:, :, 2], stats[:, :, 5], ALU.add))
            nc.vector.tensor_scalar(mean[:], mean[:], 0.5, None, ALU.mult)
            nc.vector.tensor_scalar(var[:], var[:], 1.0 / D, EPS, ALU.mult, ALU.add)
            chain(dve, nc.vector.scalar_tensor_tensor(out=mean_diff[:], in0=mean_diff[:], scalar=0.25,
                                                      in1=mean_diff[:], op0=ALU.mult, op1=ALU.mult))
            nc.vector.tensor_tensor(var[:], var[:], mean_diff[:], ALU.add).then_inc(s["var_ready"], 1)
            dve.wait_ge(s["std_ready"], 1)
            chain(dve, nc.vector.reciprocal(rstd_try[:], std[:]))
            chain(dve, nc.vector.tensor_tensor(rstd_fix[:], rstd_try[:], rstd_try[:], ALU.mult))
            chain(dve, nc.vector.tensor_tensor(rstd_fix[:], rstd_fix[:], var[:], ALU.mult))
            chain(dve, nc.vector.tensor_scalar(rstd_fix[:], rstd_fix[:], -0.5, 1.5, ALU.mult, ALU.add))
            chain(dve, nc.vector.tensor_tensor(rstd[:], rstd_try[:], rstd_fix[:], ALU.mult))
            nc.vector.scalar_tensor_tensor(out=shift[:], in0=mean[:], scalar=-1.0, in1=rstd[:], op0=ALU.mult,
                                           op1=ALU.mult).then_inc(s["shift_ready"], 1)

        def norm_vector(dve, s, src, arrives=None):
            norm_statistics(dve, s, src, arrives)
            for j in range(0, NT, 2):
                nc.vector.tensor_scalar(xn_tok[:, j * D:(j + 1) * D], src[:, j * D:(j + 1) * D], mean[:, j:j + 1],
                                        rstd[:, j:j + 1], ALU.subtract, ALU.mult).then_inc(s["xn_even"], 1)

        def norm_scalar(act, s, src):
            act.wait_ge(s["var_ready"], 1)
            nc.scalar.activation(std[:], var[:], ACT.Sqrt).then_inc(s["std_ready"], 1)
            act.wait_ge(s["shift_ready"], 1)
            for j in range(1, NT, 2):
                nc.scalar.activation(xn_tok[:, j * D:(j + 1) * D], src[:, j * D:(j + 1) * D], ACT.Identity,
                                     bias=shift[:, j:j + 1], scale=rstd[:, j:j + 1]).then_inc(s["xn_odd"], 1)

        def chain(dve, instruction):
            dve_count[0] += 1
            instruction.then_inc(dve_step, 1)
            dve.wait_ge(dve_step, dve_count[0])

        def norm_transposes(pe, s):
            for g in range(NG):
                pe.wait_ge(s["xn_even"], GROUP // 2 * (g + 1))
                pe.wait_ge(s["xn_odd"], GROUP // 2 * (g + 1))
                for k in range(GROUP):
                    j = g * GROUP + k
                    nc.tensor.transpose(psum[:, g, k * P:(k + 1) * P], xn_tok[:, j * D:(j + 1) * D],
                                        ident[:]).then_inc(s["xnT_psum"], 1)

        def norm_evacuate(act, s):
            for g in range(NG):
                act.wait_ge(s["xnT_psum"], GROUP * (g + 1))
                nc.scalar.copy(xnT[:, g * CH:(g + 1) * CH], psum[:, g, :]).then_inc(s["xnT_ready"], 1)

        def ffn_sync(sp, f):
            by_token = "(j p) d -> p j d"
            for g in range(NG):
                sp.wait_ge(f["norm"]["xn_even"], GROUP // 2 * (g + 1))
                sp.wait_ge(f["norm"]["xn_odd"], GROUP // 2 * (g + 1))
                sp.dma_start(xn_rows[g * CH:(g + 1) * CH, :].rearrange(by_token, p=P),
                             xn_tok[:, g * GROUP * D:(g + 1) * GROUP * D].rearrange("p (j d) -> p j d", d=D)
                             ).then_inc(f["xn_stored"], 16)
            sp.wait_ge(f["ys_stored"][0], 16 * (SLOT_TILES // 2 + 1))
            sp.wait_ge(f["ys_stored"][1], 16 * (SLOT_TILES // 2))
            for g in range(NG):
                sp.dma_start(y_tok[:, g * GROUP * D:(g + 1) * GROUP * D].rearrange("p (j d) -> p j d", d=D),
                             y_rows[g * CH:(g + 1) * CH, :].rearrange(by_token, p=P)).then_inc(f["y_loaded"][g], 16)

        def ffn_gpsimd(pool, f):
            def gather(t):
                if t >= 2:
                    pool.wait_ge(f["xsT_psum"], t - 1)
                nc.gpsimd.indirect_dma_start(xs_sb[:, t % 2, :], None, xn_rows,
                                             bass.IndirectOffsetOnAxis(ap=gather_row[:, t:t + 1], axis=0)
                                             ).then_inc(f["xs_loaded"][t % 2], 16)

            def scatter(t):
                pool.wait_ge(f["ys_ready"], t + 1)
                nc.gpsimd.indirect_dma_start(y_rows, bass.IndirectOffsetOnAxis(ap=scatter_row[:, t:t + 1], axis=0),
                                             ys_sb[:, t % 2, :], None).then_inc(f["ys_stored"][t % 2], 16)

            pool.wait_ge(f["xn_stored"], 16 * NG)
            pool.wait_ge(f["gather_row_ready"], 1)
            for t in range(4):
                gather(t)
            pool.wait_ge(f["scatter_row_ready"], 1)
            for t in range(SLOT_TILES):
                if t + 4 < SLOT_TILES:
                    gather(t + 4)
                scatter(t)

        def ffn_vector(dve, f):
            norm_vector(dve, f["norm"], x_tok)
            dve.wait_ge(f["logits_psum"], NT)
            router_bias = router_b_sb[:].unsqueeze(1).broadcast_to([P, NT, E])
            chain(dve, nc.vector.tensor_tensor(logits[:], psum[:, 4, 0:NT * E].rearrange("p (j e) -> p j e", e=E),
                                               router_bias, ALU.add))
            chain(dve, nc.vector.tensor_reduce(top_logit[:], logits[:], AX.X, ALU.max))
            nc.vector.tensor_tensor(logits[:], logits[:], top_logit[:].unsqueeze(2).broadcast_to([P, NT, E]),
                                    ALU.subtract).then_inc(f["sub_ready"], 1)
            dve.wait_ge(f["sub_ready"], 1)
            chain(dve, nc.vector.tensor_scalar(below_top[:], logits[:], 0.0, float(E), ALU.is_lt, ALU.mult))
            chain(dve, nc.vector.tensor_tensor(below_top[:], below_top[:], expert_iota[:], ALU.add))
            chain(dve, nc.vector.tensor_reduce(first_top[:], below_top[:], AX.X, ALU.min))
            nc.vector.tensor_tensor(chosen[:].rearrange("p e j -> p j e"), below_top[:],
                                    first_top[:].unsqueeze(2).broadcast_to([P, NT, E]),
                                    ALU.is_equal).then_inc(f["chosen_ready"], 1)
            dve.wait_ge(f["expo_ready"], 1)
            chain(dve, nc.vector.tensor_reduce(expo_sum[:], expo[:], AX.X, ALU.add))
            chain(dve, nc.vector.reciprocal(half_prob[:], expo_sum[:]))
            chain(dve, nc.vector.tensor_scalar(half_prob[:], half_prob[:], 0.5, None, ALU.mult))
            dve.wait_ge(f["prefix_psum"], 2)
            in_tile, of_tile = psum[:, 5, 0:E * NT], psum[:, 6, 0:E * NT]
            chain(dve, nc.vector.tensor_tensor_scan(upto_tile[:], scan_keep[:].rearrange("p e j -> p (e j)"),
                                                    of_tile, 0.0, ALU.mult, ALU.add))
            counts = upto_tile[:].rearrange("p (e j) -> p e j", e=E)[:, :, NT - 1]
            chain(dve, nc.vector.tensor_scalar(expert_tiles_i[:], counts, float(P - 1), None, ALU.add))
            nc.vector.tensor_tensor(upto_tile[:], upto_tile[:], of_tile, ALU.subtract)
            chain(dve, nc.vector.tensor_scalar(expert_tiles_i[:], expert_tiles_i[:], LOG_P, None, ALU.arith_shift_right))
            nc.vector.tensor_copy(expert_tiles[:], expert_tiles_i[:])
            chain(dve, nc.vector.tensor_tensor(upto_tile[:], upto_tile[:], in_tile, ALU.add))
            chain(dve, nc.vector.tensor_tensor_scan(last_tile[:], ones_e[:], expert_tiles[:], 0.0, ALU.mult, ALU.add))
            chain(dve, nc.vector.tensor_tensor(first_tile[:], last_tile[:], expert_tiles[:], ALU.subtract))
            chain(dve, nc.vector.scalar_tensor_tensor(
                out=slot_of[:], in0=first_tile[:].unsqueeze(2).broadcast_to([P, E, NT]), scalar=float(P),
                in1=upto_tile[:].rearrange("p (e j) -> p e j", e=E), op0=ALU.mult, op1=ALU.add))
            chain(dve, nc.vector.tensor_tensor(slot_of[:], slot_of[:], chosen[:], ALU.mult))
            chain(dve, nc.vector.tensor_reduce(slot_f[:], slot_of[:].rearrange("p e j -> p j e"), AX.X, ALU.add))
            chain(dve, nc.vector.tensor_copy(slot[:], slot_f[:]))
            nc.vector.tensor_scalar(slot_tile[:], slot[:], LOG_P, None, ALU.arith_shift_right)
            chain(dve, nc.vector.tensor_scalar(slot_lane[:], slot[:], P - 1, None, ALU.bitwise_and))
            chain(dve, nc.vector.tensor_tensor(
                at_tile[:, :, 0, :], slot_tile[:].unsqueeze(2).broadcast_to([P, NT, SLOT_TILES]),
                tile_iota_i[:].unsqueeze(1).broadcast_to([P, NT, SLOT_TILES]), ALU.is_equal))
            nc.vector.tensor_scalar(at_tile[:, :, 1, :], at_tile[:, :, 0, :], partition[:], None, ALU.mult)
            nc.vector.tensor_tensor(at_tile[:, :, 2, :], at_tile[:, :, 0, :],
                                    token_tile[:].unsqueeze(2).broadcast_to([P, NT, SLOT_TILES]),
                                    ALU.mult).then_inc(f["at_tile_ready"], 1)
            for g in range(NG):
                tiles = slice(g * GROUP, (g + 1) * GROUP)
                nc.vector.tensor_tensor(at_lane[:, tiles, :], slot_lane[:, tiles].unsqueeze(2).broadcast_to([P, GROUP, P]),
                                        lane_iota[:].unsqueeze(1).broadcast_to([P, GROUP, P]),
                                        ALU.is_equal).then_inc(f["at_lane_ready"], 1)
            chain(dve, nc.vector.tensor_tensor(
                tile_past[:], last_tile[0:1, :].unsqueeze(1).broadcast_to([1, SLOT_TILES, E]),
                tile_iota[0:1, :].unsqueeze(2).broadcast_to([1, SLOT_TILES, E]), ALU.is_le))
            chain(dve, nc.vector.tensor_reduce(tile_expert_f[:], tile_past[:], AX.X, ALU.add))
            nc.vector.tensor_scalar(tile_expert[:], tile_expert_f[:], float(E - 1), None,
                                    ALU.min).then_inc(f["tile_expert_ready"], 1)
            dve.wait_ge(f["info_psum"], 1)
            chain(dve, nc.vector.tensor_copy(slot_info[:].rearrange("p a t -> p (a t)"), psum[:, 7, 0:3 * SLOT_TILES]))
            nc.vector.scalar_tensor_tensor(out=gather_row[:], in0=slot_info[:, 2, :], scalar=float(P),
                                           in1=slot_info[:, 1, :], op0=ALU.mult, op1=ALU.add
                                           ).then_inc(f["gather_row_ready"], 1)
            nc.vector.scalar_tensor_tensor(out=slot_token[:], in0=slot_info[:, 2, :], scalar=float(P),
                                           in1=slot_info[:, 1, :], op0=ALU.mult, op1=ALU.add)
            chain(dve, nc.vector.tensor_scalar(spare[:], slot_info[:, 0, :], -1.0, 1.0, ALU.mult, ALU.add))
            chain(dve, nc.vector.tensor_tensor(spare[:], spare[:], spare_row[:], ALU.mult))
            nc.vector.tensor_tensor(scatter_row[:], slot_token[:], spare[:], ALU.add).then_inc(f["scatter_row_ready"], 1)

            def turn(t, k):
                dve.wait_ge(f["xsT_psum"], t + 1)
                if not isinstance(t, int) or t >= 2:
                    dve.wait_ge(f["h_g"], t - 1)
                nc.vector.tensor_copy(xsT_sb[:, k, :], psum[:, 7, k * P:(k + 1) * P]).then_inc(f["xsT_ready"], 1)

            def gate(t, k):
                dve.wait_ge(f["gate_ready"], t + 1)
                dve.wait_ge(f["h_g"], t + 1)
                if not isinstance(t, int) or t >= 2:
                    dve.wait_ge(f["uT_psum"], t - 1)
                nc.vector.tensor_tensor(u_sb[:, k, :], gate_sb[:, k, :], psum[:, 2 * k + 1, :],
                                        ALU.mult).then_inc(f["u_ready"], 1)

            def give(t, k):
                dve.wait_ge(f["ys_psum"], t + 1)
                if not isinstance(t, int) or t >= 2:
                    dve.wait_ge(f["ys_stored"][k], ys_store_count(t, k))
                nc.vector.tensor_copy(ys_sb[:, k, :], psum[:, 6, 0:D]).then_inc(f["ys_ready"], 1)

            def ys_store_count(t, k):
                return (t - k) * 8

            def step(t, k):
                turn(t, k)
                gate(t - 1, 1 - k)
                if not isinstance(t, int) or t >= 2:
                    give(t - 2, k)

            turn(0, 0)
            step(1, 1)
            with dve.Fori(1, (SLOT_TILES - 1) // 2) as i:
                dve_pair(step, i)
            step(SLOT_TILES - 1, 0)
            gate(SLOT_TILES - 1, 0)
            give(SLOT_TILES - 2, 1)
            give(SLOT_TILES - 1, 0)
            for g in range(NG):
                dve.wait_ge(f["y_loaded"][g], 16)
                for j in range(g * GROUP, (g + 1) * GROUP):
                    nc.vector.scalar_tensor_tensor(out=x_tok[:, j * D:(j + 1) * D], in0=y_tok[:, j * D:(j + 1) * D],
                                                   scalar=half_prob[:, j:j + 1], in1=x_tok[:, j * D:(j + 1) * D],
                                                   op0=ALU.mult, op1=ALU.add).then_inc(f["combined"], 1)
            dve.wait_ge(f["combined"], NT)

        def dve_pair(step, i):
            step(2 * i, 0)
            step(2 * i + 1, 1)

        def ffn_scalar(act, f):
            norm_scalar(act, f["norm"], x_tok)
            nc.scalar.preload_act_table(ACT.Exp)
            norm_evacuate(act, f["norm"])
            act.wait_ge(f["sub_ready"], 1)
            nc.scalar.activation(expo[:], logits[:], ACT.Exp).then_inc(f["expo_ready"], 1)
            nc.scalar.preload_act_table(ACT.Silu)

            def silu(t, k):
                act.wait_ge(f["h_a"], t + 1)
                if not isinstance(t, int) or t >= 2:
                    act.wait_ge(f["u_ready"], t - 1)
                nc.scalar.activation(gate_sb[:, k, :], psum[:, 2 * k, :], ACT.Silu).then_inc(f["gate_ready"], 1)

            def turned(t, k):
                act.wait_ge(f["uT_psum"], t + 1)
                if not isinstance(t, int) or t >= 2:
                    act.wait_ge(f["ys_psum"], t - 1)
                nc.scalar.copy(uT_sb[:, k, :], psum[:, 4 + k, :]).then_inc(f["uT_ready"], 1)

            def step(t, k):
                silu(t, k)
                turned(t - 1, 1 - k)

            silu(0, 0)
            step(1, 1)
            step(2, 0)
            with act.Fori(1, (SLOT_TILES - 1) // 2) as i:
                step(2 * i + 1, 1)
                step(2 * i + 2, 0)
            turned(SLOT_TILES - 1, 0)

        def ffn_tensor(pe, f):
            norm_transposes(pe, f["norm"])
            for j in range(NT):
                pe.wait_ge(f["norm"]["xnT_ready"], j // GROUP + 1)
                nc.tensor.matmul(psum[:, 4, j * E:(j + 1) * E], xnT[:, j * P:(j + 1) * P], router_sb[:],
                                 start=True, stop=True).then_inc(f["logits_psum"], 1)
            pe.wait_ge(f["chosen_ready"], 1)
            flat = chosen[:].rearrange("p e j -> p (e j)")
            nc.tensor.matmul(psum[:, 5, 0:E * NT], earlier[:], flat, start=True, stop=True).then_inc(f["prefix_psum"], 1)
            nc.tensor.matmul(psum[:, 6, 0:E * NT], ones[:], flat, start=True, stop=True).then_inc(f["prefix_psum"], 1)
            pe.wait_ge(f["at_tile_ready"], 1)
            for j in range(NT):
                pe.wait_ge(f["at_lane_ready"], j // GROUP + 1)
                last = nc.tensor.matmul(psum[:, 7, 0:3 * SLOT_TILES], at_lane[:, j, :],
                                        at_tile[:, j, :, :].rearrange("p a t -> p (a t)"),
                                        start=(j == 0), stop=(j == NT - 1))
            last.then_inc(f["info_psum"], 1)
            pe.wait_ge(loaded_w, 16 * 2 * E)
            pe.wait_ge(f["tile_expert_ready"], 1)

            def turn(t, k):
                pe.wait_ge(f["xs_loaded"][k], (t - k) * 8 + 16)
                if not isinstance(t, int) or t >= 2:
                    pe.wait_ge(f["xsT_ready"], t - 1)
                nc.tensor.transpose(psum[:, 7, k * P:(k + 1) * P], xs_sb[:, k, :], ident[:]).then_inc(f["xsT_psum"], 1)

            def expert_of(t):
                return nc.tensor.value_load(tile_expert[0:1, ds(t, 1)], min_val=0, max_val=E - 1)

            def hidden(t, k, part, e):
                bank, done = (2 * k, f["h_a"]) if part == 0 else (2 * k + 1, f["h_g"])
                if part == 0:
                    pe.wait_ge(f["xsT_ready"], t + 1)
                if not isinstance(t, int) or t >= 2:
                    if part == 0:
                        pe.wait_ge(f["gate_ready"], t - 1)
                    else:
                        pe.wait_ge(f["u_ready"], t - 1)
                nc.tensor.matmul(psum[:, bank, :], xsT_sb[:, k, :], w1_sb[:, ds(e * (2 * F) + part * F, F)],
                                 start=True, stop=True).then_inc(done, 1)

            def turn_u(t, k):
                pe.wait_ge(f["u_ready"], t + 1)
                if not isinstance(t, int) or t >= 2:
                    pe.wait_ge(f["uT_ready"], t - 1)
                for c in range(FC):
                    last = nc.tensor.transpose(psum[:, 4 + k, c * P:(c + 1) * P], u_sb[:, k, c * P:(c + 1) * P], ident[:])
                last.then_inc(f["uT_psum"], 1)

            def down(t, k, e):
                pe.wait_ge(f["uT_ready"], t + 1)
                if not isinstance(t, int) or t >= 1:
                    pe.wait_ge(f["ys_ready"], t)
                for c in range(FC):
                    last = nc.tensor.matmul(psum[:, 6, 0:D], uT_sb[:, k, c * P:(c + 1) * P],
                                            w2_sb[:, ds(e * (FC * D) + c * D, D)], start=(c == 0), stop=(c == FC - 1))
                last.then_inc(f["ys_psum"], 1)

            def step(t, k, ahead=True):
                e = expert_of(t)
                turn_u(t - 1, 1 - k)
                hidden(t, k, 1, e)
                e_before = expert_of(t - 1)
                if ahead:
                    turn(t + 1, 1 - k)
                down(t - 1, 1 - k, e_before)
                if ahead:
                    hidden(t + 1, 1 - k, 0, expert_of(t + 1))

            turn(0, 0)
            e = expert_of(0)
            hidden(0, 0, 0, e)
            hidden(0, 0, 1, e)
            turn(1, 1)
            hidden(1, 1, 0, expert_of(1))
            step(1, 1)
            step(2, 0)
            with pe.Fori(1, (SLOT_TILES - 3) // 2) as i:
                step(2 * i + 1, 1)
                step(2 * i + 2, 0)
            step(SLOT_TILES - 2, 1)
            step(SLOT_TILES - 1, 0, ahead=False)
            turn_u(SLOT_TILES - 1, 0)
            down(SLOT_TILES - 1, 0, expert_of(SLOT_TILES - 1))

        with nc.Block() as block:
            @block.sync
            def _(sp):
                sp.dma_start(x_tok[:].rearrange("p (j d) -> p j d", d=D),
                             x_in.rearrange("b (j p) d -> p (b j) d", p=P)).then_inc(loaded_x, 16)
                sp.dma_start(router_sb[:], router_w).then_inc(loaded_small, 16)
                sp.dma_start(router_b_sb[:], router_b.partition_broadcast(P)).then_inc(loaded_small, 16)
                for e in range(E):
                    sp.dma_start(w1_sb[:, e * 2 * F:(e + 1) * 2 * F], w1[e]).then_inc(loaded_w, 16)
                    sp.dma_start(w2_sb[:, e * FC * D:(e + 1) * FC * D].rearrange("p (c d) -> p c d", c=FC),
                                 w2[e].rearrange("(c p) d -> p c d", p=P)).then_inc(loaded_w, 16)
                for dst, src in (
                        (W_in_sb[:], W_in), (W_dt_sb[0:R, :], W_dt), (W_dt_sb[R:R + 1, :], b_dt.unsqueeze(0)),
                        (W_out_sb[:], W_out.rearrange("(h p) d -> p h d", p=P)),
                        (W_dtr_sb[:], W_x[:, 0:R].rearrange("(h p) r -> p h r", p=P)),
                        (W_bc_sb[:, :, 0, :], W_x[:, R:R + 2 * S].rearrange("(h p) r -> p h r", p=P)),
                        (W_bc_sb[:, :, 1, :], W_x[:, R:R + 2 * S].rearrange("(h p) r -> p h r", p=P)),
                        (W_bc_sb[:, :, 2, :], W_x[:, R:R + 2 * S].rearrange("(h p) r -> p h r", p=P)),
                        (conv_w_sb[:], conv_w.rearrange("(h p) k -> p h k", p=P)),
                        (A_sb[:], A_log.rearrange("(h p) s -> p h s", p=P)),
                        *((t[:, h:h + 1], v[h * P:(h + 1) * P].unsqueeze(1)) for h in range(NH)
                          for t, v in ((conv_b_sb, conv_b), (D_skip_sb, D_skip))),
                        (ln_g_sb[:], ln_g.partition_broadcast(P)), (ln_b_sb[:], ln_b.partition_broadcast(P))):
                    sp.dma_start(dst, src).then_inc(loaded_m, 16)
                ffn_sync(sp, FF[0])

            @block.gpsimd
            def _(pool):
                def then(instruction):
                    pool_count[0] += 1
                    instruction.then_inc(pool_step, 1)
                    pool.wait_ge(pool_step, pool_count[0])

                then(nc.gpsimd.memset(ident[:], 0.0))
                then(nc.gpsimd.affine_select(out=ident[:], in_=ident[:], compare_op=ALU.not_equal, fill=1.0, base=0,
                                             pattern=[[-1, P]], channel_multiplier=1))
                then(nc.gpsimd.memset(ones[:], 1.0))
                then(nc.gpsimd.affine_select(out=earlier[:], in_=ones[:], compare_op=ALU.is_ge, fill=0.0, base=-1,
                                             pattern=[[1, P]], channel_multiplier=-1))
                nc.gpsimd.iota(expert_iota_i[:], [[0, NT], [1, E]], base=0, channel_multiplier=0)
                nc.gpsimd.iota(tile_iota_i[:], [[1, SLOT_TILES]], base=0, channel_multiplier=0)
                nc.gpsimd.iota(lane_iota[:], [[1, P]], base=0, channel_multiplier=0)
                nc.gpsimd.iota(token_tile_i[:], [[1, NT]], base=0, channel_multiplier=0)
                nc.gpsimd.iota(partition_i[:], [[0, 1]], base=0, channel_multiplier=1)
                then(nc.gpsimd.iota(spare_row_i[:], [[P, SLOT_TILES]], base=N, channel_multiplier=1))
                nc.gpsimd.tensor_copy(expert_iota[:], expert_iota_i[:])
                nc.gpsimd.tensor_copy(tile_iota[:], tile_iota_i[:])
                nc.gpsimd.tensor_copy(token_tile[:], token_tile_i[:])
                nc.gpsimd.tensor_copy(partition[:], partition_i[:])
                nc.gpsimd.tensor_copy(spare_row[:], spare_row_i[:])
                nc.gpsimd.memset(ones_e[:], 1.0)
                then(nc.gpsimd.memset(scan_keep[:], 1.0))
                then(nc.gpsimd.memset(scan_keep[:, :, 0:1], 0.0))
                then(nc.gpsimd.memset(pick_row[:], 0.0))
                for part in range(3):
                    then(nc.gpsimd.affine_select(out=pick_row[:], in_=pick_row[:], compare_op=ALU.not_equal, fill=1.0,
                                                 base=-2 * S * part, pattern=[[-1, 2 * S]], channel_multiplier=1))
                nc.gpsimd.memset(bc_parts[:, N:N + CH], 0.0).then_inc(consts_ready, 1)
                ffn_gpsimd(pool, FF[0])

            @block.vector
            def _(dve):
                dve.wait_ge(loaded_x, 16)
                dve.wait_ge(loaded_small, 32)
                dve.wait_ge(consts_ready, 1)
                ffn_vector(dve, FF[0])

            @block.scalar
            def _(act):
                ffn_scalar(act, FF[0])

            @block.tensor
            def _(pe):
                pe.wait_ge(loaded_small, 32)
                pe.wait_ge(consts_ready, 1)
                ffn_tensor(pe, FF[0])

        with nc.Block() as block:
            chunk = [slice(c * CH, (c + 1) * CH) for c in range(NC)]

            @block.sync
            def _(sp):
                pass

            @block.gpsimd
            def _(pool):
                nc.gpsimd.memset(dt_rank[R:R + 1, :, :], 1.0).then_inc(M["pads_clear"], 1)
                pool.wait_ge(M["pads_clear"], 1)
                nc.gpsimd.memset(xc_pre[:, :, :, 0:PAD], 0.0).then_inc(M["pads_clear"], 1)
                pool.wait_ge(M["norm"]["xn_even"], NT // 2)
                pool.wait_ge(M["norm"]["xn_odd"], NT // 2)
                for half in range(2):
                    rows = x_tok[:, half * N // 2:(half + 1) * N // 2].rearrange("p (j d) -> p j d", d=D)
                    nc.gpsimd.tensor_tensor(rows, rows, ln_b_sb[:].unsqueeze(1).broadcast_to([P, NT // 2, D]),
                                            ALU.add).then_inc(M["x_plus_b"], 1)
                for c in range(NC):
                    k = c % 2
                    pool.wait_ge(M["round_ready"], c + 1)
                    nc.gpsimd.tensor_tensor(soft_err[:, k], soft_exp[:, k], soft_err[:, k],
                                            ALU.subtract).then_inc(M["err_ready"], 1)
                    pool.wait_ge(M["soft_ln_ready"], c + 1)
                    pool.wait_ge(M["err_ready"], c + 1)
                    nc.gpsimd.tensor_tensor(soft_ln[:, k], soft_ln[:, k], soft_err[:, k],
                                            ALU.add).then_inc(M["lnerr_ready"], 1)

            @block.vector
            def _(dve):
                dve.wait_ge(loaded_m, 16 * M_LOADS)
                norm_vector(dve, M["norm"], x_tok)
                for h in range(NH):
                    nc.vector.tensor_scalar(D_diag[:, h, :], ident[:], D_skip_sb[:, h:h + 1], None, ALU.mult)
                dve.wait_ge(M["A_exp"], 1)
                nc.vector.tensor_scalar(neg_A[:], A_sb[:].rearrange("p h s -> p (h s)"), -1.0, None, ALU.mult
                                        ).then_inc(M["neg_A_ready"], 1)
                dve.wait_ge(M["pads_clear"], 2)
                for c in range(NC):
                    b, q = divmod(c, CPB)
                    dve.wait_ge(M["xc_pre_ready"], c + 1)
                    for tap in range(TAPS):
                        for h in range(NH):
                            shifted = xc_pre[:, h, b, q * CH + tap:q * CH + tap + CH]
                            w = conv_w_sb[:, h, tap:tap + 1]
                            if tap == 0:
                                step = nc.vector.tensor_scalar(xc[:, h, chunk[c]], shifted, w, None, ALU.mult)
                            else:
                                dve.wait_ge(M["conv_step"], NH * (TAPS * c + tap - 1) + h + 1)
                                step = nc.vector.scalar_tensor_tensor(
                                    out=xc[:, h, chunk[c]], in0=shifted, scalar=w, in1=xc[:, h, chunk[c]],
                                    op0=ALU.mult, op1=ALU.add)
                            step.then_inc(M["conv_step"], 1)
                for c in range(NC):
                    k = c % 2
                    dve.wait_ge(M["bc1_ready"], c + 1)
                    if c >= 2:
                        dve.wait_ge(M["bc3_ready"], c - 1)
                        dve.wait_ge(M["lnerr_ready"], c - 1)
                    nc.vector.tensor_tensor(bc_rest[:, k, :], psum[0:64, 4 * k + 1, :], bc_parts[0:64, chunk[c]],
                                            ALU.subtract).then_inc(M["bc_rest_ready"], 1)
                    dve.wait_ge(M["soft_exp_ready"], c + 1)
                    nc.vector.tensor_scalar(soft_err[:, k], soft_exp[:, k], 1.0, -1.0, ALU.add, ALU.add
                                            ).then_inc(M["round_ready"], 1)
                    dve.wait_ge(M["bc2_ready"], c + 1)
                    nc.vector.tensor_tensor(bc_parts[0:32, chunk[c]], bc_rest[0:32, k, :], bc_parts[0:32, chunk[c]],
                                            ALU.subtract).then_inc(M["bc3_ready"], 1)
                    dve.wait_ge(M["lnerr_ready"], c + 1)
                    nc.vector.scalar_tensor_tensor(out=dt[:, :, chunk[c]], in0=psum[:, 4 * k + 2:4 * k + 4, :], scalar=0.0,
                                                   in1=soft_ln[:, k], op0=ALU.max, op1=ALU.add).then_inc(M["dt_ready"], 1)
                    dve.wait_ge(M["dt_ready"], c + 1)
                    nc.vector.tensor_tensor(dtx[:, :, chunk[c]], dt[:, :, chunk[c]], xc[:, :, chunk[c]], ALU.mult
                                            ).then_inc(M["dtx_ready"], 1)

            @block.scalar
            def _(act):
                act.wait_ge(loaded_m, 16 * M_LOADS)
                nc.scalar.activation(A_sb[:], A_sb[:], ACT.Exp).then_inc(M["A_exp"], 1)
                norm_scalar(act, M["norm"], x_tok)
                nc.scalar.preload_act_table(ACT.Silu)
                norm_evacuate(act, M["norm"])

                def hold(c):
                    b, q = divmod(c, CPB)
                    act.wait_ge(M["xc_psum"], c + 1)
                    nc.scalar.copy(xc_pre[:, :, b, PAD + q * CH:PAD + (q + 1) * CH],
                                   psum[:, 4 * (c % 2):4 * (c % 2) + NH, :]).then_inc(M["xc_pre_ready"], 1)

                def silu_gate(c):
                    act.wait_ge(M["z_psum"], c + 1)
                    nc.scalar.activation(silu_z[:, :, chunk[c]], psum[:, 4 * (c % 2) + NH:4 * (c % 2) + 2 * NH, :],
                                         ACT.Silu).then_inc(M["silu_z_ready"], 1)

                def silu_conv(c):
                    for h in range(NH):
                        act.wait_ge(M["conv_step"], NH * (TAPS * c + TAPS - 1) + h + 1)
                        nc.scalar.activation(xc[:, h, chunk[c]], xc[:, h, chunk[c]], ACT.Silu,
                                             bias=conv_b_sb[:, h:h + 1]).then_inc(M["xc_ready"], 1)

                hold(0)
                hold(1)
                for c in range(NC):
                    silu_gate(c)
                    if c + 2 < NC:
                        hold(c + 2)
                for c in range(NC):
                    silu_conv(c)

                nc.scalar.preload_act_table_set("natural_log_exp_and_others")

                def ranks(c):
                    k = c % 2
                    act.wait_ge(M["proj_psum"], 2 * c + 1)
                    if c >= 2:
                        act.wait_ge(M["v_psum"], c - 1)
                    nc.scalar.copy(dt_rank[0:R, k, :], psum[0:R, 4 * k, :]).then_inc(M["dtr_ready"], 1)
                    act.wait_ge(M["proj_psum"], 2 * c + 2)
                    nc.scalar.copy(bc_parts[:, chunk[c]], psum[0:96, 4 * k + 1, :]).then_inc(M["bc1_ready"], 1)

                ranks(0)
                for c in range(NC):
                    k = c % 2
                    if c + 1 < NC:
                        ranks(c + 1)
                    act.wait_ge(M["v_psum"], c + 1)
                    if c >= 2:
                        act.wait_ge(M["err_ready"], c - 1)
                        act.wait_ge(M["dt_ready"], c - 1)
                    nc.scalar.activation(soft_exp[:, k], psum[:, 4 * k + 2:4 * k + 4, :], ACT.Abs
                                         ).then_inc(M["soft_abs_ready"], 1)
                    act.wait_ge(M["soft_abs_ready"], c + 1)
                    nc.scalar.activation(soft_exp[:, k], soft_exp[:, k], ACT.Exp, scale=-1.0
                                         ).then_inc(M["soft_exp_ready"], 1)
                    act.wait_ge(M["soft_exp_ready"], c + 1)
                    nc.scalar.activation(soft_ln[:, k], soft_exp[:, k], ACT.Ln, bias=1.0).then_inc(M["soft_ln_ready"], 1)
                    act.wait_ge(M["bc_rest_ready"], c + 1)
                    nc.scalar.copy(bc_parts[0:64, chunk[c]], bc_rest[:, k, :]).then_inc(M["bc2_ready"], 1)

            @block.tensor
            def _(pe):
                pe.wait_ge(loaded_m, 16 * M_LOADS)
                norm_transposes(pe, M["norm"])

                def inner(c, z):
                    pe.wait_ge(M["norm"]["xnT_ready"], NG)
                    if c >= 2:
                        pe.wait_ge(M["silu_z_ready"] if z else M["xc_pre_ready"], c - 1)
                    for h in range(NH):
                        m = z * NH + h
                        mm = nc.tensor.matmul(psum[:, 4 * (c % 2) + m, :], W_in_sb[:, m * P:(m + 1) * P],
                                              xnT[:, chunk[c]], start=True, stop=True)
                    mm.then_inc(M["z_psum"] if z else M["xc_psum"], 1)

                inner(0, 0)
                inner(1, 0)
                for c in range(NC):
                    inner(c, 1)
                    if c + 2 < NC:
                        inner(c + 2, 0)

                def project(c):
                    pe.wait_ge(M["xc_ready"], NH * (c + 1))
                    pe.wait_ge(M["xc_pre_ready"], NC)
                    if c >= 2:
                        pe.wait_ge(M["dtr_ready"], c - 1)
                        pe.wait_ge(M["bc_rest_ready"], c - 1)
                    for m, rows in ((0, R), (1, 96)):
                        for h in range(NH):
                            lhsT = W_bc_sb[:, h].rearrange("p a b -> p (a b)") if m else W_dtr_sb[:, h, :]
                            mm = nc.tensor.matmul(psum[0:rows, 4 * (c % 2) + m, :], lhsT, xc[:, h, chunk[c]],
                                                  start=(h == 0), stop=(h == NH - 1))
                        mm.then_inc(M["proj_psum"], 1)

                def delta(c):
                    pe.wait_ge(M["dtr_ready"], c + 1)
                    pe.wait_ge(M["silu_z_ready"], NC)
                    pe.wait_ge(M["pads_clear"], 1)
                    if c >= 2:
                        pe.wait_ge(M["dt_ready"], c - 1)
                    for h in range(NH):
                        mm = nc.tensor.matmul(psum[:, 4 * (c % 2) + 2 + h, :], W_dt_sb[:, h * P:(h + 1) * P],
                                              dt_rank[:, c % 2, :], start=True, stop=True)
                    mm.then_inc(M["v_psum"], 1)

                project(0)
                for c in range(1, NC):
                    project(c)
                    delta(c - 1)
                delta(NC - 1)

        with nc.Block() as block:
            dA_bank = [psum[:, h, :] for h in range(NH)]
            C_bank = [psum[:, 2 + k, :] for k in range(2)]
            B_bank = psum[:, 4, :]
            y_bank = [psum[:, 5 + h, :] for h in range(NH)]
            o_bank = psum[:, 7, :]
            POOL_GROUP = NG - 1

            def scale_rows(engine, g, done):
                rows = xn_tok[:, g * GROUP * D:(g + 1) * GROUP * D].rearrange("p (j d) -> p j d", d=D)
                engine.tensor_tensor(rows, rows, ln_g_sb[:].unsqueeze(1).broadcast_to([P, GROUP, D]),
                                     ALU.mult).then_inc(done, 1)

            def add_rows(engine, g, done):
                rows = slice(g * GROUP * D, (g + 1) * GROUP * D)
                engine.tensor_tensor(x_tok[:, rows], x_tok[:, rows], xn_tok[:, rows], ALU.add).then_inc(done, 1)

            @block.sync
            def _(sp):
                pass

            @block.gpsimd
            def _(pool):
                def step(k, c, parity):
                    pool.wait_ge(M["B_ready"], k + 1)
                    pool.wait_ge(M["scan_done"], 2 * k + 2)
                    nc.gpsimd.tensor_tensor(dBx[:, parity], dtx[:, :, chunk[c]],
                                            B_sb[:, parity:parity + 1, :].broadcast_to([P, NH, CH]),
                                            ALU.mult).then_inc(M["dBx_ready"], 1)

                for c in range(NC):
                    with pool.Fori(0, S // 2) as i:
                        for parity in range(2):
                            step(c * S + 2 * i + parity, c, parity)
                pool.wait_ge(M["out_norm"]["xn_even"], GROUP // 2 * (POOL_GROUP + 1))
                pool.wait_ge(M["out_norm"]["xn_odd"], GROUP // 2 * (POOL_GROUP + 1))
                scale_rows(nc.gpsimd, POOL_GROUP, M["scale_ready_pool"])
                pool.wait_ge(M["scale_ready_pool"], 1)
                add_rows(nc.gpsimd, POOL_GROUP, M["x_ready_pool"])
                pool.wait_ge(M["x_ready_pool"], 1)

            @block.vector
            def _(dve):
                nc.vector.sem_inc(M["scan_done"], 4)
                nc.vector.sem_inc(M["hC_ready"], 2)

                def scans(k, s, parity):
                    dve.wait_ge(M["dBx_ready"], k + 1)
                    dve.wait_ge(M["carry_ready"], k + 1)
                    dve.wait_ge(M["hC_ready"], k + 1)
                    for h in range(NH):
                        dve.wait_ge(M["dA_ready"], 2 * k + h + 1)
                        nc.vector.tensor_tensor_scan(H[:, parity, h, :], dA_bank[h], dBx[:, parity, h, :],
                                                     carry[:, ds(s * NH + h, 1)],
                                                     ALU.mult, ALU.add).then_inc(M["scan_done"], 1)

                def product(k, parity):
                    dve.wait_ge(M["C_psum"], k + 1)
                    dve.wait_ge(M["sum_done"], k + 1)
                    dve.wait_ge(M["scan_done"], 2 * k + 6)
                    nc.vector.tensor_tensor(hC[:, parity], H[:, parity],
                                            C_bank[parity].unsqueeze(1).broadcast_to([P, NH, CH]),
                                            ALU.mult).then_inc(M["hC_ready"], 1)

                def gate(c):
                    dve.wait_ge(M["y_ready"], c + 1)
                    if c >= 1:
                        dve.wait_ge(M["o_psum"], c * GROUP)
                    nc.vector.tensor_tensor(yz, y_sb, silu_z[:, :, chunk[c]], ALU.mult).then_inc(M["yz_ready"], 1)

                for c in range(NC):
                    first = c * S
                    if c % CPB == 0:
                        dve.wait_ge(M["carry_ready"], first + 2)
                        nc.vector.memset(carry[:], 0.0).then_inc(M["carry_clear"], 1)
                        dve.wait_ge(M["carry_clear"], c // CPB + 1)
                    for s in range(2):
                        scans(first + s, s, s % 2)
                        if first + s >= 1:
                            product(first + s - 1, 1 - s % 2)
                    with dve.Fori(1, S // 2) as i:
                        for parity in range(2):
                            s = 2 * i + parity
                            scans(first + s, s, parity)
                            product(first + s - 1, 1 - parity)
                    if c >= 1:
                        gate(c - 1)
                product(NC * S - 1, 1)
                gate(NC - 1)
                norm_vector(dve, M["out_norm"], y_tok, arrives=(M["o_ready"], 1))
                dve.wait_ge(M["x_plus_b"], 2)
                for g in range(POOL_GROUP):
                    dve.wait_ge(M["out_norm"]["xn_even"], GROUP // 2 * (g + 1))
                    dve.wait_ge(M["out_norm"]["xn_odd"], GROUP // 2 * (g + 1))
                    scale_rows(nc.vector, g, M["scale_ready"])
                for g in range(POOL_GROUP):
                    dve.wait_ge(M["scale_ready"], g + 1)
                    add_rows(nc.vector, g, M["x_ready"])
                dve.wait_ge(M["x_ready"], POOL_GROUP)

            @block.scalar
            def _(act):
                def spread(k, parity):
                    act.wait_ge(M["B_psum"], k + 1)
                    if not isinstance(k, int) or k >= 2:
                        act.wait_ge(M["dBx_ready"], k - 1)
                    nc.scalar.copy(B_sb[:, parity, :], B_bank).then_inc(M["B_ready"], 1)

                def decay(k, c, s):
                    for h in range(NH):
                        act.wait_ge(M["scan_done"], 2 * k + 3 + h)
                        nc.scalar.activation(dA_bank[h], dt[:, h, chunk[c]], ACT.Exp,
                                             scale=neg_A[:, ds(s + h * S, 1)]).then_inc(M["dA_ready"], 1)

                def keep(k, s, parity):
                    act.wait_ge(M["scan_done"], 2 * k + 6)
                    nc.scalar.copy(carry[:, ds(s * NH, NH)], H[:, parity, :, CH - 1]).then_inc(M["carry_ready"], 1)

                def leave(c):
                    act.wait_ge(M["sum_done"], (c + 1) * S + 2)
                    if c >= 1:
                        act.wait_ge(M["yz_ready"], c)
                    nc.scalar.copy(y_sb, psum[:, 5:5 + NH, :]).then_inc(M["y_ready"], 1)

                def rows_out(c):
                    act.wait_ge(M["o_psum"], (c + 1) * GROUP)
                    nc.scalar.copy(y_tok[:, c * GROUP * D:(c + 1) * GROUP * D], o_bank).then_inc(M["o_ready"], 1)

                nc.scalar.sem_inc(M["carry_ready"], 2)
                spread(0, 0)
                spread(1, 1)
                PEEL = 4
                for c in range(NC):
                    first = c * S
                    for s in range(PEEL):
                        decay(first + s, c, s)
                        if first + s >= 1:
                            keep(first + s - 1, (s - 1) % S, 1 - s % 2)
                        spread(first + s + 2, s % 2)
                        if s == 1 and c >= 1:
                            leave(c - 1)
                    with act.Fori(PEEL // 2, S // 2) as i:
                        for parity in range(2):
                            s = 2 * i + parity
                            decay(first + s, c, s)
                            keep(first + s - 1, s - 1, 1 - parity)
                            spread(first + s + 2, parity)
                    if c >= 2:
                        rows_out(c - 2)
                leave(NC - 1)
                rows_out(NC - 2)
                rows_out(NC - 1)
                norm_scalar(act, M["out_norm"], y_tok)

            @block.tensor
            def _(pe):
                def spread(bank, row, c, done):
                    nc.tensor.matmul(bank, pick_row[:, ds(row, 1)].broadcast_to([96, P]),
                                     bc_parts[:, c * CH:(c + 1) * CH], start=True, stop=True).then_inc(done, 1)

                def step(k, parity, C_next, B_next, c=0, first=False, last=False):
                    pe.wait_ge(M["B_ready"], k + 3)
                    spread(B_bank, B_next[1], B_next[0], M["B_psum"])
                    pe.wait_ge(M["hC_ready"], k + 3)
                    spread(C_bank[parity], S + C_next[1], C_next[0], M["C_psum"])
                    if first:
                        if c >= 1:
                            pe.wait_ge(M["y_ready"], c)
                        for h in range(NH):
                            nc.tensor.matmul(y_bank[h], D_diag[:, h, :], xc[:, h, chunk[c]], start=True, stop=False)
                    for h in range(NH):
                        mm = nc.tensor.matmul(y_bank[h], ident[:], hC[:, parity, h, :], start=False, stop=last)
                    mm.then_inc(M["sum_done"], 1)

                def project(c):
                    pe.wait_ge(M["yz_ready"], c + 1)
                    if c >= 1:
                        pe.wait_ge(M["o_ready"], c)
                    for t in range(GROUP):
                        for h in range(NH):
                            mm = nc.tensor.matmul(o_bank[:, t * D:(t + 1) * D], yz[:, h, t * P:(t + 1) * P],
                                                  W_out_sb[:, h, :], start=(h == 0), stop=(h == NH - 1))
                        mm.then_inc(M["o_psum"], 1)

                nc.tensor.sem_inc(M["sum_done"], 2)
                spread(B_bank, 0, 0, M["B_psum"])
                spread(C_bank[0], S, 0, M["C_psum"])
                spread(C_bank[1], S + 1, 0, M["C_psum"])
                for n in (1, 2):
                    pe.wait_ge(M["B_ready"], n)
                    spread(B_bank, n, 0, M["B_psum"])
                AHEAD = 4
                for c in range(NC):
                    k = c * S
                    for s in range(2):
                        step(k + s, s % 2, (c, s + 2), (c, s + 3), c, first=(s == 0))
                    with pe.Fori(1, (S - AHEAD) // 2) as i:
                        for parity in range(2):
                            s = 2 * i + parity
                            step(k + s, parity, (c, s + 2), (c, s + 3))
                    for s in range(S - AHEAD, S):
                        step(k + s, s % 2, (c + (s + 2) // S, (s + 2) % S), (c + (s + 3) // S, (s + 3) % S),
                             last=(s == S - 1))
                    if c >= 1:
                        project(c - 1)
                project(NC - 1)

        with nc.Block() as block:
            @block.sync
            def _(sp):
                ffn_sync(sp, FF[1])
                sp.wait_ge(FF[1]["combined"], NT)
                sp.dma_start(out.rearrange("b (j p) d -> p (b j) d", p=P),
                             x_tok[:].rearrange("p (j d) -> p j d", d=D)).then_inc(out_stored, 16)
                sp.wait_ge(out_stored, 16)

            @block.gpsimd
            def _(pool):
                ffn_gpsimd(pool, FF[1])

            @block.vector
            def _(dve):
                ffn_vector(dve, FF[1])

            @block.scalar
            def _(act):
                ffn_scalar(act, FF[1])

            @block.tensor
            def _(pe):
                ffn_tensor(pe, FF[1])


_NAMES = ["attn_x", "attn_W_in", "attn_conv_w", "attn_conv_b", "attn_W_x", "attn_W_dt", "attn_b_dt", "attn_A_log",
          "attn_D_skip", "attn_W_out", "attn_ln_g", "attn_ln_b", "ffn_router_w", "ffn_router_b", "ffn_w1", "ffn_w2"]


def kernel(**inputs):
    import numpy as np
    import concourse.bacc as bacc
    from concourse.bass_utils import run_bass_kernel_spmd

    nc = bacc.Bacc("TRN2", target_bir_lowering=False, num_devices=1)
    arrays, args = {}, []
    for name in _NAMES:
        a = np.ascontiguousarray(inputs["L0_" + name])
        arrays[name] = a
        args.append(nc.dram_tensor(name, a.shape, mybir.dt.from_np(a.dtype), kind="ExternalInput").ap())
    shape = inputs["L0_attn_x"].shape
    args.append(nc.dram_tensor("out", shape, F32, kind="ExternalOutput").ap())
    macaron_kernel(nc, *args)
    r = run_bass_kernel_spmd(nc, [arrays], core_ids=[0])
    return r.results[0]["out"]
```

```python
from contextlib import ExitStack

import concourse.bass as bass
from concourse import mybir

ALU = mybir.AluOpType
ACT = mybir.ActivationFunctionType
AX = mybir.AxisListType
F32 = mybir.dt.float32
BF16 = mybir.dt.bfloat16
I32 = mybir.dt.int32
U32 = mybir.dt.uint32

P = 128
EPS = 1e-5


GROUP = 4


def macaron_kernel(nc, x_in, W_in, conv_w, conv_b, W_x, W_dt, b_dt, A_log, D_skip, W_out, ln_g, ln_b,
                   router_w, router_b, w1, w2, out):
    B, L, D = x_in.shape
    N = B * L
    NT = N // P
    NG = NT // GROUP
    E = router_w.shape[1]
    F = w2.shape[1]
    FC = F // P
    DI = W_out.shape[0]
    NH = DI // P
    S = A_log.shape[1]
    TAPS = conv_w.shape[1]
    R = W_dt.shape[0]
    FIRST, SECOND, THIRD = R, R + 2 * S, R - 2 * S
    assert SECOND + 2 * S == P and THIRD % 32 == 0
    CH = 512
    NC = N // CH
    CPB = L // CH
    SLOT_TILES = (N + E * (P - 1)) // P
    PAD = TAPS - 1
    LOG_P = P.bit_length() - 1
    M_LOADS = 10 + 2 * NH
    ds = bass.ds
    assert D == P and NH == 2 and E == 8 and 2 * S == 32 and SLOT_TILES % 2 == 1

    with ExitStack() as ctx:
        def sb(name, shape, dt=F32):
            return ctx.enter_context(nc.sbuf_tensor(name, shape, dt))

        def sem(name):
            return ctx.enter_context(nc.semaphore(name))

        xn_rows = nc.dram_tensor("xn_rows", (N, D), F32).ap()
        y_rows = nc.dram_tensor("y_rows", (N + SLOT_TILES * P, D), F32).ap()

        ident = sb("ident", [P, P])
        earlier = sb("earlier", [P, P], BF16)
        ones = sb("ones", [P, P], BF16)
        expert_iota_i = sb("expert_iota_i", [P, NT, E], I32)
        expert_iota = sb("expert_iota", [P, NT, E])
        tile_iota_i = sb("tile_iota_i", [P, SLOT_TILES], I32)
        tile_iota = sb("tile_iota", [P, SLOT_TILES])
        lane_iota = sb("lane_iota", [P, P], I32)
        token_tile_i = sb("token_tile_i", [P, NT], I32)
        token_tile = sb("token_tile", [P, NT])
        partition_i = sb("partition_i", [P, 1], I32)
        partition = sb("partition", [P, 1])
        spare_row_i = sb("spare_row_i", [P, SLOT_TILES], I32)
        spare_row = sb("spare_row", [P, SLOT_TILES])
        scan_keep = sb("scan_keep", [P, E, NT])
        ones_e = sb("ones_e", [P, E])
        pick_row = sb("pick_row", [P, 2 * S], BF16)

        w1_sb = sb("w1_sb", [P, E * 2 * F])
        w2_sb = sb("w2_sb", [P, E * FC * D])
        router_sb = sb("router_sb", [P, E])
        router_b_sb = sb("router_b_sb", [P, E])
        W_in_sb = sb("W_in_sb", [P, 2 * DI])
        W_x_sb = sb("W_x_sb", [P, NH, P])
        W_dt_sb = sb("W_dt_sb", [R + 1, DI])
        W_out_sb = sb("W_out_sb", [P, NH, D])
        conv_w_sb = sb("conv_w_sb", [P, NH, TAPS])
        conv_b_sb = sb("conv_b_sb", [P, NH])
        D_skip_sb = sb("D_skip_sb", [P, NH])
        D_diag = sb("D_diag", [P, NH, P])
        A_sb = sb("A_sb", [P, NH, S])
        neg_A = sb("neg_A", [P, NH * S])
        ln_g_sb = sb("ln_g_sb", [P, D])
        ln_b_sb = sb("ln_b_sb", [P, D])

        x_tok = sb("x_tok", [P, NT * D])
        xn_tok = sb("xn_tok", [P, NT * D])
        xnT = sb("xnT", [P, N])
        y_tok = xnT

        stats = sb("stats", [P, NT, 6])
        mean = sb("mean", [P, NT])
        mean_diff = sb("mean_diff", [P, NT])
        var = sb("var", [P, NT])
        std = sb("std", [P, NT])
        rstd_try = sb("rstd_try", [P, NT])
        rstd_fix = sb("rstd_fix", [P, NT])
        rstd = sb("rstd", [P, NT])
        shift = sb("shift", [P, NT])

        logits = sb("logits", [P, NT, E])
        top_logit = sb("top_logit", [P, NT])
        expo = sb("expo", [P, NT, E])
        expo_sum = sb("expo_sum", [P, NT])
        half_prob = sb("half_prob", [P, NT])
        below_top = sb("below_top", [P, NT, E])
        first_top = sb("first_top", [P, NT])
        chosen = sb("chosen", [P, E, NT], BF16)
        upto_tile = sb("upto_tile", [P, E * NT])
        expert_tiles_i = sb("expert_tiles_i", [P, E], I32)
        expert_tiles = sb("expert_tiles", [P, E])
        last_tile = sb("last_tile", [P, E])
        first_tile = sb("first_tile", [P, E])
        slot_of = sb("slot_of", [P, E, NT])
        slot_f = sb("slot_f", [P, NT])
        slot = sb("slot", [P, NT], I32)
        slot_tile = sb("slot_tile", [P, NT], I32)
        slot_lane = sb("slot_lane", [P, NT], I32)
        slot_info = sb("slot_info", [P, 3, SLOT_TILES])
        slot_token = sb("slot_token", [P, SLOT_TILES])
        spare = sb("spare", [P, SLOT_TILES])
        gather_row = sb("gather_row", [P, SLOT_TILES], U32)
        scatter_row = sb("scatter_row", [P, SLOT_TILES], U32)
        tile_past = sb("tile_past", [1, SLOT_TILES, E])
        tile_expert_f = sb("tile_expert_f", [1, SLOT_TILES])
        tile_expert = sb("tile_expert", [1, SLOT_TILES], I32)

        SLOTS = 4
        phase = sb("phase", [P, NH * B * (PAD + L) + 16 * CH])

        def carve(*shapes):
            views, at = [], 0
            for rows, *dims in shapes:
                size = 1
                for n in dims:
                    size *= n
                flat = phase[0:rows, at:at + size]
                names = "abc"[:len(dims)]
                if len(dims) > 1:
                    flat = flat.rearrange(f"p ({' '.join(names)}) -> p {' '.join(names)}", **dict(zip(names, dims)))
                views.append(flat)
                at += size
            assert at <= phase.shape[1]
            return views

        xs_sb, xsT_sb, w1_tile, gate_sb, u_sb, ys_sb, lanes, tiles3 = carve(
            (P, 2, D), (P, 2, P), (P, 2, 2 * F), (P, 2, F), (P, 2, F), (P, 2, D), (P, NT * P // 2),
            (P, NT * 3 * SLOT_TILES // 2))
        at_lane = lanes.bitcast(BF16).rearrange("p (j m) -> p j m", m=P)
        at_tile = tiles3.bitcast(BF16).rearrange("p (j a t) -> p j a t", a=3, t=SLOT_TILES)
        xc_pre, dt_rank, soft_exp, bc_rest = carve(
            (P, NH, B, PAD + L), (R + 1, 2, CH), (P, NC, NH, CH), (P, NC, CH))
        H, B_sb, dBx, hC, y_sb, yz = carve(
            (P, SLOTS, NH, CH), (P, 2, CH), (P, 2, NH, CH), (P, 2, NH, CH), (P, NH, CH), (P, NH, CH))

        xc = sb("xc", [P, NH, N])
        silu_z = sb("silu_z", [P, NH, N])
        dt = sb("dt", [P, NH, N])
        dtx = sb("dtx", [P, NH, N])
        carry = sb("carry", [P, S * NH])
        bc_parts = sb("bc_parts", [P, N + CH], BF16)

        psum = ctx.enter_context(nc.psum_tensor("psum", [P, 8, 512], F32))

        loaded_x = sem("loaded_x")
        loaded_small = sem("loaded_small")
        loaded_w = sem("loaded_w")
        loaded_m = sem("loaded_m")
        ident_ready = sem("ident_ready")
        consts_ready = sem("consts_ready")
        pool_step = sem("pool_step")
        dve_step = sem("dve_step")
        out_stored = sem("out_stored")
        pool_count, dve_count = [0], [0]

        def norm_sems(tag):
            return {n: sem(f"{tag}_{n}") for n in (
                "stats_done", "var_ready", "std_ready", "shift_ready", "xn_even", "xn_odd", "xnT_psum", "xnT_even", "xnT_odd")}

        def ffn_sems(tag):
            f = {n: sem(f"{tag}_{n}") for n in (
                "logits_psum", "sub_ready", "expo_ready", "chosen_ready", "prefix_psum", "at_tile_ready",
                "at_lane_ready", "info_psum", "gather_row_ready", "scatter_row_ready", "tile_expert_ready", "xn_stored",
                "xsT_psum", "xsT_ready", "w1_ready", "h_a", "h_g", "gate_ready", "u_ready", "ys_psum",
                "ys_ready", "combined")}
            f["y_loaded"] = [sem(f"{tag}_y_loaded{g}") for g in range(NG)]
            f["xs_loaded"] = [sem(f"{tag}_xs_loaded{k}") for k in range(2)]
            f["ys_stored"] = [sem(f"{tag}_ys_stored{k}") for k in range(2)]
            f["norm"] = norm_sems(tag)
            return f

        FF = [ffn_sems("ffn0"), ffn_sems("ffn1")]
        M = {n: sem(f"m_{n}") for n in (
            "A_exp", "neg_A_ready", "pads_clear", "xc_psum", "z_psum", "xc_pre_ready", "silu_z_ready", "conv_step",
            "xc_ready", "proj_psum", "dtr_ready", "v_psum", "soft_abs_ready", "soft_exp_ready", "soft_ln_ready",
            "round_ready", "err_ready", "log_ready", "last_err_ready", "last_log_ready", "dt_ready", "dtx_ready", "bc1_ready", "bc_full_ready", "bc_rest_ready",
            "bc2_ready", "bc3_ready", "x_plus_b", "B_psum", "B_ready", "C_psum", "dBx_ready", "hC_ready",
            "sum_done", "carry_clear", "carry_ready", "y_ready", "yz_ready", "o_psum", "o_ready",
            "scale_ready", "x_ready", "scale_ready_pool", "x_ready_pool")}
        M["scan_done"] = [sem(f"m_scan_done{h}") for h in range(NH)]
        M["dA_ready"] = [sem(f"m_dA_ready{h}") for h in range(NH)]
        M["norm"] = norm_sems("m")
        M["out_norm"] = norm_sems("mo")

        def norm_statistics(dve, s, src, arrives):
            for j in range(NT):
                if arrives and j % GROUP == 0:
                    signal, by_group = arrives
                    dve.wait_ge(signal, by_group * (j // GROUP + 1))
                last = nc.vector.bn_stats(stats[:, j, :], src[:, j * D:(j + 1) * D])
            last.then_inc(s["stats_done"], 1)
            dve.wait_ge(s["stats_done"], 1)
            mean_even, mean_odd = stats[:, :, 1], stats[:, :, 4]
            nc.vector.tensor_tensor(mean_diff[:], mean_even, mean_odd, ALU.subtract)
            nc.vector.tensor_tensor(mean[:], mean_even, mean_odd, ALU.add)
            chain(dve, nc.vector.tensor_tensor(var[:], stats[:, :, 2], stats[:, :, 5], ALU.add))
            nc.vector.tensor_scalar(mean[:], mean[:], 0.5, None, ALU.mult)
            nc.vector.tensor_scalar(var[:], var[:], 1.0 / D, EPS, ALU.mult, ALU.add)
            chain(dve, nc.vector.scalar_tensor_tensor(out=mean_diff[:], in0=mean_diff[:], scalar=0.25,
                                                      in1=mean_diff[:], op0=ALU.mult, op1=ALU.mult))
            nc.vector.tensor_tensor(var[:], var[:], mean_diff[:], ALU.add).then_inc(s["var_ready"], 1)
            dve.wait_ge(s["std_ready"], 1)
            chain(dve, nc.vector.reciprocal(rstd_try[:], std[:]))
            chain(dve, nc.vector.tensor_tensor(rstd_fix[:], rstd_try[:], rstd_try[:], ALU.mult))
            chain(dve, nc.vector.tensor_tensor(rstd_fix[:], rstd_fix[:], var[:], ALU.mult))
            chain(dve, nc.vector.tensor_scalar(rstd_fix[:], rstd_fix[:], -0.5, 1.5, ALU.mult, ALU.add))
            chain(dve, nc.vector.tensor_tensor(rstd[:], rstd_try[:], rstd_fix[:], ALU.mult))
            nc.vector.scalar_tensor_tensor(out=shift[:], in0=mean[:], scalar=-1.0, in1=rstd[:], op0=ALU.mult,
                                           op1=ALU.mult).then_inc(s["shift_ready"], 1)

        def norm_vector(dve, s, src, arrives=None):
            norm_statistics(dve, s, src, arrives)
            for j in range(0, NT, 2):
                nc.vector.tensor_scalar(xn_tok[:, j * D:(j + 1) * D], src[:, j * D:(j + 1) * D], mean[:, j:j + 1],
                                        rstd[:, j:j + 1], ALU.subtract, ALU.mult).then_inc(s["xn_even"], 1)

        def norm_scalar(act, s, src, next_function=None):
            nc.scalar.preload_act_table(ACT.Sqrt)
            act.wait_ge(s["var_ready"], 1)
            nc.scalar.activation(std[:], var[:], ACT.Sqrt).then_inc(s["std_ready"], 1)
            if next_function is not None:
                nc.scalar.preload_act_table(next_function)
            act.wait_ge(s["shift_ready"], 1)
            for j in range(1, NT, 2):
                nc.scalar.activation(xn_tok[:, j * D:(j + 1) * D], src[:, j * D:(j + 1) * D], ACT.Identity,
                                     bias=shift[:, j:j + 1], scale=rstd[:, j:j + 1]).then_inc(s["xn_odd"], 1)

        def chain(dve, instruction):
            dve_count[0] += 1
            instruction.then_inc(dve_step, 1)
            dve.wait_ge(dve_step, dve_count[0])

        def norm_transposes(pe, s, bank):
            for g in range(NG):
                pe.wait_ge(s["xn_even"], GROUP // 2 * (g + 1))
                pe.wait_ge(s["xn_odd"], GROUP // 2 * (g + 1))
                for k in range(GROUP):
                    j = g * GROUP + k
                    nc.tensor.transpose(psum[:, bank + g, k * P:(k + 1) * P], xn_tok[:, j * D:(j + 1) * D],
                                        ident[:]).then_inc(s["xnT_psum"], 1)

        def pool_chain(pool, instruction):
            pool_count[0] += 1
            instruction.then_inc(pool_step, 1)
            pool.wait_ge(pool_step, pool_count[0])

        def wait_xnT(pe, s, g):
            pe.wait_ge(s["xnT_odd" if g % 2 else "xnT_even"], g // 2 + 1)

        def norm_evacuate(engine, copy, s, bank, groups, done):
            for g in groups:
                engine.wait_ge(s["xnT_psum"], GROUP * (g + 1))
                copy(xnT[:, g * CH:(g + 1) * CH], psum[:, bank + g, :]).then_inc(done, 1)

        def ffn_sync(sp, f):
            by_token = "(j p) d -> p j d"
            for g in range(NG):
                sp.wait_ge(f["norm"]["xn_even"], GROUP // 2 * (g + 1))
                sp.wait_ge(f["norm"]["xn_odd"], GROUP // 2 * (g + 1))
                sp.dma_start(xn_rows[g * CH:(g + 1) * CH, :].rearrange(by_token, p=P),
                             xn_tok[:, g * GROUP * D:(g + 1) * GROUP * D].rearrange("p (j d) -> p j d", d=D)
                             ).then_inc(f["xn_stored"], 16)
            sp.wait_ge(f["ys_stored"][0], 16 * (SLOT_TILES // 2 + 1))
            sp.wait_ge(f["ys_stored"][1], 16 * (SLOT_TILES // 2))
            for g in range(NG):
                sp.dma_start(y_tok[:, g * GROUP * D:(g + 1) * GROUP * D].rearrange("p (j d) -> p j d", d=D),
                             y_rows[g * CH:(g + 1) * CH, :].rearrange(by_token, p=P)).then_inc(f["y_loaded"][g], 16)

        def ffn_gpsimd(pool, f):
            def gather(t):
                if t >= 2:
                    pool.wait_ge(f["xsT_psum"], t - 1)
                nc.gpsimd.indirect_dma_start(xs_sb[:, t % 2, :], None, xn_rows,
                                             bass.IndirectOffsetOnAxis(ap=gather_row[:, t:t + 1], axis=0)
                                             ).then_inc(f["xs_loaded"][t % 2], 16)

            def scatter(t):
                pool.wait_ge(f["ys_ready"], t + 1)
                nc.gpsimd.indirect_dma_start(y_rows, bass.IndirectOffsetOnAxis(ap=scatter_row[:, t:t + 1], axis=0),
                                             ys_sb[:, t % 2, :], None).then_inc(f["ys_stored"][t % 2], 16)

            pool.wait_ge(f["xn_stored"], 16 * NG)
            pool.wait_ge(f["gather_row_ready"], 1)
            for t in range(4):
                gather(t)
            pool.wait_ge(f["scatter_row_ready"], 1)
            for t in range(SLOT_TILES):
                if t + 4 < SLOT_TILES:
                    gather(t + 4)
                scatter(t)

        def ffn_vector(dve, f):
            norm_vector(dve, f["norm"], x_tok)
            norm_evacuate(dve, nc.vector.tensor_copy, f["norm"], 0, range(1, NG, 2), f["norm"]["xnT_odd"])
            dve.wait_ge(loaded_small, 32)
            dve.wait_ge(consts_ready, 1)
            dve.wait_ge(f["logits_psum"], NT)
            router_bias = router_b_sb[:].unsqueeze(1).broadcast_to([P, NT, E])
            top = top_logit[:].unsqueeze(2).broadcast_to([P, NT, E])
            chain(dve, nc.vector.tensor_tensor(logits[:], psum[:, 4, 0:NT * E].rearrange("p (j e) -> p j e", e=E),
                                               router_bias, ALU.add))
            chain(dve, nc.vector.tensor_reduce(top_logit[:], logits[:], AX.X, ALU.max))
            chain(dve, nc.vector.tensor_tensor(below_top[:], logits[:], top, ALU.is_lt))
            chain(dve, nc.vector.scalar_tensor_tensor(out=below_top[:], in0=below_top[:], scalar=float(E),
                                                      in1=expert_iota[:], op0=ALU.mult, op1=ALU.add))
            chain(dve, nc.vector.tensor_reduce(first_top[:], below_top[:], AX.X, ALU.min))
            nc.vector.tensor_tensor(chosen[:].rearrange("p e j -> p j e"), below_top[:],
                                    first_top[:].unsqueeze(2).broadcast_to([P, NT, E]),
                                    ALU.is_equal).then_inc(f["chosen_ready"], 1)
            nc.vector.tensor_tensor(logits[:], logits[:], top, ALU.subtract).then_inc(f["sub_ready"], 1)
            dve.wait_ge(f["prefix_psum"], 2)
            in_tile, of_tile = psum[:, 5, 0:E * NT], psum[:, 6, 0:E * NT]
            chain(dve, nc.vector.tensor_tensor_scan(upto_tile[:], scan_keep[:].rearrange("p e j -> p (e j)"),
                                                    of_tile, 0.0, ALU.mult, ALU.add))
            counts = upto_tile[:].rearrange("p (e j) -> p e j", e=E)[:, :, NT - 1]
            chain(dve, nc.vector.tensor_scalar(expert_tiles_i[:], counts, float(P - 1), None, ALU.add))
            nc.vector.tensor_tensor(upto_tile[:], upto_tile[:], of_tile, ALU.subtract)
            chain(dve, nc.vector.tensor_scalar(expert_tiles_i[:], expert_tiles_i[:], LOG_P, None, ALU.arith_shift_right))
            nc.vector.tensor_copy(expert_tiles[:], expert_tiles_i[:])
            chain(dve, nc.vector.tensor_tensor(upto_tile[:], upto_tile[:], in_tile, ALU.add))
            chain(dve, nc.vector.tensor_tensor_scan(last_tile[:], ones_e[:], expert_tiles[:], 0.0, ALU.mult, ALU.add))
            chain(dve, nc.vector.tensor_tensor(first_tile[:], last_tile[:], expert_tiles[:], ALU.subtract))
            chain(dve, nc.vector.scalar_tensor_tensor(
                out=slot_of[:], in0=first_tile[:].unsqueeze(2).broadcast_to([P, E, NT]), scalar=float(P),
                in1=upto_tile[:].rearrange("p (e j) -> p e j", e=E), op0=ALU.mult, op1=ALU.add))
            chain(dve, nc.vector.tensor_tensor(slot_of[:], slot_of[:], chosen[:], ALU.mult))
            chain(dve, nc.vector.tensor_reduce(slot_f[:], slot_of[:].rearrange("p e j -> p j e"), AX.X, ALU.add))
            chain(dve, nc.vector.tensor_copy(slot[:], slot_f[:]))
            nc.vector.tensor_scalar(slot_tile[:], slot[:], LOG_P, None, ALU.arith_shift_right)
            chain(dve, nc.vector.tensor_scalar(slot_lane[:], slot[:], P - 1, None, ALU.bitwise_and))
            chain(dve, nc.vector.tensor_tensor(
                at_tile[:, :, 0, :], slot_tile[:].unsqueeze(2).broadcast_to([P, NT, SLOT_TILES]),
                tile_iota_i[:].unsqueeze(1).broadcast_to([P, NT, SLOT_TILES]), ALU.is_equal))
            nc.vector.tensor_scalar(at_tile[:, :, 1, :], at_tile[:, :, 0, :], partition[:], None, ALU.mult)
            nc.vector.tensor_tensor(at_tile[:, :, 2, :], at_tile[:, :, 0, :],
                                    token_tile[:].unsqueeze(2).broadcast_to([P, NT, SLOT_TILES]),
                                    ALU.mult).then_inc(f["at_tile_ready"], 1)
            for g in range(NG):
                tiles = slice(g * GROUP, (g + 1) * GROUP)
                nc.vector.tensor_tensor(at_lane[:, tiles, :], slot_lane[:, tiles].unsqueeze(2).broadcast_to([P, GROUP, P]),
                                        lane_iota[:].unsqueeze(1).broadcast_to([P, GROUP, P]),
                                        ALU.is_equal).then_inc(f["at_lane_ready"], 1)
            dve.wait_ge(f["info_psum"], 1)
            chain(dve, nc.vector.tensor_copy(slot_info[:].rearrange("p a t -> p (a t)"), psum[:, 7, 0:3 * SLOT_TILES]))
            nc.vector.scalar_tensor_tensor(out=gather_row[:], in0=slot_info[:, 2, :], scalar=float(P),
                                           in1=slot_info[:, 1, :], op0=ALU.mult, op1=ALU.add
                                           ).then_inc(f["gather_row_ready"], 1)
            chain(dve, nc.vector.tensor_tensor(
                tile_past[:], last_tile[0:1, :].unsqueeze(1).broadcast_to([1, SLOT_TILES, E]),
                tile_iota[0:1, :].unsqueeze(2).broadcast_to([1, SLOT_TILES, E]), ALU.is_le))
            chain(dve, nc.vector.tensor_reduce(tile_expert_f[:], tile_past[:], AX.X, ALU.add))
            nc.vector.tensor_scalar(tile_expert[:], tile_expert_f[:], float(E - 1), None,
                                    ALU.min).then_inc(f["tile_expert_ready"], 1)
            nc.vector.scalar_tensor_tensor(out=slot_token[:], in0=slot_info[:, 2, :], scalar=float(P),
                                           in1=slot_info[:, 1, :], op0=ALU.mult, op1=ALU.add)
            chain(dve, nc.vector.tensor_scalar(spare[:], slot_info[:, 0, :], -1.0, 1.0, ALU.mult, ALU.add))
            chain(dve, nc.vector.tensor_tensor(spare[:], spare[:], spare_row[:], ALU.mult))
            nc.vector.tensor_tensor(scatter_row[:], slot_token[:], spare[:], ALU.add).then_inc(f["scatter_row_ready"], 1)

            dve.wait_ge(f["expo_ready"], 1)
            chain(dve, nc.vector.tensor_reduce(expo_sum[:], expo[:], AX.X, ALU.add))
            chain(dve, nc.vector.reciprocal(half_prob[:], expo_sum[:]))
            chain(dve, nc.vector.tensor_scalar(half_prob[:], half_prob[:], 0.5, None, ALU.mult))

            def pick(t, k):
                e = nc.vector.value_load(tile_expert[0:1, ds(t, 1)], min_val=0, max_val=E - 1)
                if not isinstance(t, int) or t >= 2:
                    dve.wait_ge(f["h_g"], t - 1)
                nc.vector.tensor_copy(w1_tile[:, k, :], w1_sb[:, ds(e * (2 * F), 2 * F)]).then_inc(f["w1_ready"], 1)

            def gate(t, k):
                dve.wait_ge(f["gate_ready"], t + 1)
                dve.wait_ge(f["h_g"], t + 1)
                if not isinstance(t, int) or t >= 2:
                    dve.wait_ge(f["ys_psum"], t - 1)
                nc.vector.tensor_tensor(u_sb[:, k, :], gate_sb[:, k, :], psum[:, 2 * k + 1, :],
                                        ALU.mult).then_inc(f["u_ready"], 1)

            def step(t, k):
                pick(t + 1, 1 - k)
                gate(t, k)

            dve.wait_ge(f["tile_expert_ready"], 1)
            dve.wait_ge(loaded_w, 16 * 2 * E)
            pick(0, 0)
            step(0, 0)
            step(1, 1)
            with dve.Fori(1, (SLOT_TILES - 1) // 2) as i:
                step(2 * i, 0)
                step(2 * i + 1, 1)
            gate(SLOT_TILES - 1, 0)
            for g in range(NG):
                dve.wait_ge(f["y_loaded"][g], 16)
                for j in range(g * GROUP, (g + 1) * GROUP):
                    nc.vector.scalar_tensor_tensor(out=x_tok[:, j * D:(j + 1) * D], in0=y_tok[:, j * D:(j + 1) * D],
                                                   scalar=half_prob[:, j:j + 1], in1=x_tok[:, j * D:(j + 1) * D],
                                                   op0=ALU.mult, op1=ALU.add).then_inc(f["combined"], 1)
            dve.wait_ge(f["combined"], NT)

        def ffn_scalar(act, f):
            norm_scalar(act, f["norm"], x_tok, ACT.Exp)
            norm_evacuate(act, nc.scalar.copy, f["norm"], 0, range(0, NG, 2), f["norm"]["xnT_even"])
            act.wait_ge(f["sub_ready"], 1)
            nc.scalar.activation(expo[:], logits[:], ACT.Exp).then_inc(f["expo_ready"], 1)
            nc.scalar.preload_act_table(ACT.Silu)

            def silu(t, k):
                act.wait_ge(f["h_a"], t + 1)
                if not isinstance(t, int) or t >= 2:
                    act.wait_ge(f["u_ready"], t - 1)
                nc.scalar.activation(gate_sb[:, k, :], psum[:, 2 * k, :], ACT.Silu).then_inc(f["gate_ready"], 1)

            def turn(t, k):
                act.wait_ge(f["xsT_psum"], t + 1)
                if not isinstance(t, int) or t >= 2:
                    act.wait_ge(f["h_g"], t - 1)
                nc.scalar.copy(xsT_sb[:, k, :], psum[:, 7, k * P:(k + 1) * P]).then_inc(f["xsT_ready"], 1)

            def give(t, k):
                act.wait_ge(f["ys_psum"], t + 1)
                if not isinstance(t, int) or t >= 2:
                    act.wait_ge(f["ys_stored"][k], (t - k) * 8)
                nc.scalar.copy(ys_sb[:, k, :], psum[:, 6, 0:D]).then_inc(f["ys_ready"], 1)

            def step(t, k):
                silu(t, k)
                if not isinstance(t, int) or t + 1 < SLOT_TILES:
                    turn(t + 1, 1 - k)
                if not isinstance(t, int) or t >= 1:
                    give(t - 1, 1 - k)

            turn(0, 0)
            for t in range(4):
                step(t, t % 2)
            with act.Fori(2, (SLOT_TILES - 1) // 2) as i:
                step(2 * i, 0)
                step(2 * i + 1, 1)
            step(SLOT_TILES - 1, 0)
            give(SLOT_TILES - 1, 0)

        def ffn_tensor(pe, f):
            norm_transposes(pe, f["norm"], 0)
            pe.wait_ge(loaded_small, 32)
            for j in range(NT):
                wait_xnT(pe, f["norm"], j // GROUP)
                nc.tensor.matmul(psum[:, 4, j * E:(j + 1) * E], xnT[:, j * P:(j + 1) * P], router_sb[:],
                                 start=True, stop=True).then_inc(f["logits_psum"], 1)
            pe.wait_ge(f["chosen_ready"], 1)
            pe.wait_ge(consts_ready, 1)
            flat = chosen[:].rearrange("p e j -> p (e j)")
            nc.tensor.matmul(psum[:, 5, 0:E * NT], earlier[:], flat, start=True, stop=True).then_inc(f["prefix_psum"], 1)
            nc.tensor.matmul(psum[:, 6, 0:E * NT], ones[:], flat, start=True, stop=True).then_inc(f["prefix_psum"], 1)
            pe.wait_ge(f["at_tile_ready"], 1)
            for j in range(NT):
                pe.wait_ge(f["at_lane_ready"], j // GROUP + 1)
                last = nc.tensor.matmul(psum[:, 7, 0:3 * SLOT_TILES], at_lane[:, j, :],
                                        at_tile[:, j, :, :].rearrange("p a t -> p (a t)"),
                                        start=(j == 0), stop=(j == NT - 1))
            last.then_inc(f["info_psum"], 1)
            pe.wait_ge(loaded_w, 16 * 2 * E)
            pe.wait_ge(f["tile_expert_ready"], 1)

            def turn(t, k):
                pe.wait_ge(f["xs_loaded"][k], (t - k) * 8 + 16)
                if not isinstance(t, int) or t >= 2:
                    pe.wait_ge(f["xsT_ready"], t - 1)
                nc.tensor.transpose(psum[:, 7, k * P:(k + 1) * P], xs_sb[:, k, :], ident[:]).then_inc(f["xsT_psum"], 1)

            def hidden(t, k, part):
                if part == 0:
                    pe.wait_ge(f["xsT_ready"], t + 1)
                    pe.wait_ge(f["w1_ready"], t + 1)
                if not isinstance(t, int) or t >= 2:
                    pe.wait_ge(f["u_ready" if part else "gate_ready"], t - 1)
                for c in range(FC):
                    last = nc.tensor.matmul(psum[:, 2 * k + part, c * P:(c + 1) * P],
                                            w1_tile[:, k, part * F + c * P:part * F + (c + 1) * P],
                                            xsT_sb[:, k, :], start=True, stop=True)
                last.then_inc(f["h_g" if part else "h_a"], 1)

            def down(t, k):
                e = nc.tensor.value_load(tile_expert[0:1, ds(t, 1)], min_val=0, max_val=E - 1)
                pe.wait_ge(f["u_ready"], t + 1)
                if not isinstance(t, int) or t >= 1:
                    pe.wait_ge(f["ys_ready"], t)
                for c in range(FC):
                    last = nc.tensor.matmul(psum[:, 6, 0:D], u_sb[:, k, c * P:(c + 1) * P],
                                            w2_sb[:, ds(e * (FC * D) + c * D, D)], start=(c == 0), stop=(c == FC - 1))
                last.then_inc(f["ys_psum"], 1)

            def step(t, k):
                hidden(t, k, 0)
                hidden(t, k, 1)
                if not isinstance(t, int) or t + 1 < SLOT_TILES:
                    turn(t + 1, 1 - k)
                if not isinstance(t, int) or t >= 1:
                    down(t - 1, 1 - k)

            turn(0, 0)
            for t in range(2):
                step(t, t % 2)
            with pe.Fori(1, (SLOT_TILES - 1) // 2) as i:
                step(2 * i, 0)
                step(2 * i + 1, 1)
            step(SLOT_TILES - 1, 0)
            down(SLOT_TILES - 1, 0)

        with nc.Block() as block:
            @block.sync
            def _(sp):
                sp.dma_start(x_tok[:].rearrange("p (j d) -> p j d", d=D),
                             x_in.rearrange("b (j p) d -> p (b j) d", p=P)).then_inc(loaded_x, 16)
                sp.dma_start(router_sb[:], router_w).then_inc(loaded_small, 16)
                sp.dma_start(router_b_sb[:], router_b.partition_broadcast(P)).then_inc(loaded_small, 16)
                for e in range(E):
                    sp.dma_start(w1_sb[:, e * 2 * F:(e + 1) * 2 * F], w1[e]).then_inc(loaded_w, 16)
                    sp.dma_start(w2_sb[:, e * FC * D:(e + 1) * FC * D].rearrange("p (c d) -> p c d", c=FC),
                                 w2[e].rearrange("(c p) d -> p c d", p=P)).then_inc(loaded_w, 16)
                for dst, src in (
                        (W_in_sb[:], W_in), (W_dt_sb[0:R, :], W_dt), (W_dt_sb[R:R + 1, :], b_dt.unsqueeze(0)),
                        (W_out_sb[:], W_out.rearrange("(h p) d -> p h d", p=P)),
                        (W_x_sb[:, :, 0:SECOND], W_x.rearrange("(h p) r -> p h r", p=P)),
                        (W_x_sb[:, :, SECOND:P], W_x[:, R:R + 2 * S].rearrange("(h p) r -> p h r", p=P)),
                        (conv_w_sb[:], conv_w.rearrange("(h p) k -> p h k", p=P)),
                        (A_sb[:], A_log.rearrange("(h p) s -> p h s", p=P)),
                        *((t[:, h:h + 1], v[h * P:(h + 1) * P].unsqueeze(1)) for h in range(NH)
                          for t, v in ((conv_b_sb, conv_b), (D_skip_sb, D_skip))),
                        (ln_g_sb[:], ln_g.partition_broadcast(P)), (ln_b_sb[:], ln_b.partition_broadcast(P))):
                    sp.dma_start(dst, src).then_inc(loaded_m, 16)
                ffn_sync(sp, FF[0])

            @block.gpsimd
            def _(pool):
                pool_chain(pool, nc.gpsimd.memset(ident[:], 0.0))
                nc.gpsimd.affine_select(out=ident[:], in_=ident[:], compare_op=ALU.not_equal, fill=1.0, base=0,
                                        pattern=[[-1, P]], channel_multiplier=1).then_inc(ident_ready, 1)
                pool.wait_ge(ident_ready, 1)
                pool_chain(pool, nc.gpsimd.memset(ones[:], 1.0))
                pool_chain(pool, nc.gpsimd.affine_select(out=earlier[:], in_=ones[:], compare_op=ALU.is_ge, fill=0.0, base=-1,
                                             pattern=[[1, P]], channel_multiplier=-1))
                nc.gpsimd.iota(expert_iota_i[:], [[0, NT], [1, E]], base=0, channel_multiplier=0)
                nc.gpsimd.iota(tile_iota_i[:], [[1, SLOT_TILES]], base=0, channel_multiplier=0)
                nc.gpsimd.iota(lane_iota[:], [[1, P]], base=0, channel_multiplier=0)
                nc.gpsimd.iota(token_tile_i[:], [[1, NT]], base=0, channel_multiplier=0)
                nc.gpsimd.iota(partition_i[:], [[0, 1]], base=0, channel_multiplier=1)
                pool_chain(pool, nc.gpsimd.iota(spare_row_i[:], [[P, SLOT_TILES]], base=N, channel_multiplier=1))
                nc.gpsimd.tensor_copy(expert_iota[:], expert_iota_i[:])
                nc.gpsimd.tensor_copy(tile_iota[:], tile_iota_i[:])
                nc.gpsimd.tensor_copy(token_tile[:], token_tile_i[:])
                nc.gpsimd.tensor_copy(partition[:], partition_i[:])
                nc.gpsimd.tensor_copy(spare_row[:], spare_row_i[:])
                nc.gpsimd.memset(ones_e[:], 1.0)
                pool_chain(pool, nc.gpsimd.memset(scan_keep[:], 1.0))
                nc.gpsimd.memset(scan_keep[:, :, 0:1], 0.0).then_inc(consts_ready, 1)
                ffn_gpsimd(pool, FF[0])

            @block.vector
            def _(dve):
                dve.wait_ge(loaded_x, 16)
                ffn_vector(dve, FF[0])

            @block.scalar
            def _(act):
                ffn_scalar(act, FF[0])

            @block.tensor
            def _(pe):
                pe.wait_ge(ident_ready, 1)
                ffn_tensor(pe, FF[0])

        with nc.Block() as block:
            chunk = [slice(c * CH, (c + 1) * CH) for c in range(NC)]

            def give_back(engine, namespace, c, err_ready, log_ready, count):
                engine.wait_ge(M["round_ready"], c + 1)
                namespace.tensor_tensor(dtx[:, :, chunk[c]], soft_exp[:, c], dtx[:, :, chunk[c]],
                                        ALU.subtract).then_inc(err_ready, 1)
                engine.wait_ge(M["soft_ln_ready"], c + 1)
                engine.wait_ge(err_ready, count)
                namespace.tensor_tensor(dt[:, :, chunk[c]], dt[:, :, chunk[c]], dtx[:, :, chunk[c]],
                                        ALU.add).then_inc(log_ready, 1)

            v_banks = [psum[:, 2 * ((c + 1) % NC):2 * ((c + 1) % NC) + NH, :] for c in range(NC)]

            @block.sync
            def _(sp):
                pass

            @block.gpsimd
            def _(pool):
                nc.gpsimd.memset(dt_rank[R:R + 1, :, :], 1.0).then_inc(M["pads_clear"], 1)
                pool.wait_ge(M["pads_clear"], 1)
                nc.gpsimd.memset(xc_pre[:, :, :, 0:PAD], 0.0).then_inc(M["pads_clear"], 1)
                pool.wait_ge(M["pads_clear"], 2)
                pool_chain(pool, nc.gpsimd.memset(pick_row[:], 0.0))
                for part in (FIRST, SECOND, THIRD):
                    pool_chain(pool, nc.gpsimd.affine_select(out=pick_row[:], in_=pick_row[:], compare_op=ALU.not_equal, fill=1.0,
                                                 base=-part, pattern=[[-1, 2 * S]], channel_multiplier=1))
                pool_chain(pool, nc.gpsimd.memset(bc_parts[0:THIRD, 0:N], 0.0))
                pool_chain(pool, nc.gpsimd.memset(bc_parts[:, N:N + CH], 0.0))
                pool.wait_ge(M["norm"]["xn_even"], NT // 2)
                pool.wait_ge(M["norm"]["xn_odd"], NT // 2)
                for half in range(2):
                    rows = x_tok[:, half * N // 2:(half + 1) * N // 2].rearrange("p (j d) -> p j d", d=D)
                    nc.gpsimd.tensor_tensor(rows, rows, ln_b_sb[:].unsqueeze(1).broadcast_to([P, NT // 2, D]),
                                            ALU.add).then_inc(M["x_plus_b"], 1)
                for c in range(NC - 1):
                    give_back(pool, nc.gpsimd, c, M["err_ready"], M["log_ready"], c + 1)

            @block.vector
            def _(dve):
                dve.wait_ge(loaded_m, 16 * M_LOADS)
                norm_vector(dve, M["norm"], x_tok)
                for h in range(NH):
                    nc.vector.tensor_scalar(D_diag[:, h, :], ident[:], D_skip_sb[:, h:h + 1], None, ALU.mult)
                norm_evacuate(dve, nc.vector.tensor_copy, M["norm"], NG, range(1, NG, 2), M["norm"]["xnT_odd"])
                dve.wait_ge(M["pads_clear"], 2)
                for c in range(NC):
                    b, q = divmod(c, CPB)
                    dve.wait_ge(M["xc_pre_ready"], c + 1)
                    for tap in range(TAPS):
                        for h in range(NH):
                            shifted = xc_pre[:, h, b, q * CH + tap:q * CH + tap + CH]
                            w = conv_w_sb[:, h, tap:tap + 1]
                            if tap == 0:
                                step = nc.vector.tensor_scalar(xc[:, h, chunk[c]], shifted, w, None, ALU.mult)
                            else:
                                dve.wait_ge(M["conv_step"], NH * (TAPS * c + tap - 1) + h + 1)
                                step = nc.vector.scalar_tensor_tensor(
                                    out=xc[:, h, chunk[c]], in0=shifted, scalar=w, in1=xc[:, h, chunk[c]],
                                    op0=ALU.mult, op1=ALU.add)
                            step.then_inc(M["conv_step"], 1)
                def rest(c):
                    dve.wait_ge(M["bc_full_ready"], c + 1)
                    nc.vector.tensor_tensor(bc_rest[SECOND:P, c, :], bc_rest[SECOND:P, c, :], bc_parts[SECOND:P, chunk[c]],
                                            ALU.subtract).then_inc(M["bc_rest_ready"], 1)

                def third(c):
                    dve.wait_ge(M["bc2_ready"], c + 1)
                    nc.vector.tensor_tensor(bc_parts[THIRD:FIRST, chunk[c]], bc_rest[SECOND:P, c, :],
                                            bc_parts[SECOND:P, chunk[c]], ALU.subtract).then_inc(M["bc3_ready"], 1)

                def rounded(c):
                    dve.wait_ge(M["soft_exp_ready"], c + 1)
                    nc.vector.tensor_scalar(dtx[:, :, chunk[c]], soft_exp[:, c], 1.0, -1.0, ALU.add, ALU.add
                                            ).then_inc(M["round_ready"], 1)

                def delta(c, log_ready, log_count, n):
                    dve.wait_ge(log_ready, log_count)
                    nc.vector.scalar_tensor_tensor(out=dt[:, :, chunk[c]], in0=v_banks[c], scalar=0.0,
                                                   in1=dt[:, :, chunk[c]], op0=ALU.max, op1=ALU.add
                                                   ).then_inc(M["dt_ready"], 1)
                    dve.wait_ge(M["dt_ready"], n)
                    nc.vector.tensor_tensor(dtx[:, :, chunk[c]], dt[:, :, chunk[c]], xc[:, :, chunk[c]], ALU.mult
                                            ).then_inc(M["dtx_ready"], 1)

                LAST = NC - 1
                rest(0)
                rest(1)
                rounded(0)
                rest(2)
                rounded(1)
                rest(LAST)
                delta(0, M["log_ready"], 1, 1)
                third(0)
                third(1)
                rounded(2)
                rounded(LAST)
                delta(1, M["log_ready"], 2, 2)
                give_back(dve, nc.vector, LAST, M["last_err_ready"], M["last_log_ready"], 1)
                third(2)
                third(LAST)
                delta(LAST, M["last_log_ready"], 1, 3)
                dve.wait_ge(M["A_exp"], 1)
                nc.vector.tensor_scalar(neg_A[:], A_sb[:].rearrange("p h s -> p (h s)"), -1.0, None, ALU.mult
                                        ).then_inc(M["neg_A_ready"], 1)
                delta(2, M["log_ready"], 3, 4)

            @block.scalar
            def _(act):
                act.wait_ge(loaded_m, 16 * M_LOADS)
                norm_scalar(act, M["norm"], x_tok, ACT.Silu)
                norm_evacuate(act, nc.scalar.copy, M["norm"], NG, range(0, NG, 2), M["norm"]["xnT_even"])

                def hold(c):
                    b, q = divmod(c, CPB)
                    act.wait_ge(M["xc_psum"], c + 1)
                    nc.scalar.copy(xc_pre[:, :, b, PAD + q * CH:PAD + (q + 1) * CH],
                                   psum[:, 2 * (c % 2):2 * (c % 2) + NH, :]).then_inc(M["xc_pre_ready"], 1)

                def silu_gate(c):
                    act.wait_ge(M["z_psum"], c + 1)
                    nc.scalar.activation(silu_z[:, :, chunk[c]], psum[:, NG + 2 * (c % 2):NG + 2 * (c % 2) + NH, :],
                                         ACT.Silu).then_inc(M["silu_z_ready"], 1)

                def silu_conv(c):
                    for h in range(NH):
                        act.wait_ge(M["conv_step"], NH * (TAPS * c + TAPS - 1) + h + 1)
                        nc.scalar.activation(xc[:, h, chunk[c]], xc[:, h, chunk[c]], ACT.Silu,
                                             bias=conv_b_sb[:, h:h + 1]).then_inc(M["xc_ready"], 1)

                def ranks(c):
                    act.wait_ge(M["proj_psum"], c + 1)
                    if c >= 2:
                        act.wait_ge(M["v_psum"], c - 1)
                    nc.scalar.copy(dt_rank[0:R, c % 2, :], psum[0:R, c % 2, :]).then_inc(M["dtr_ready"], 1)
                    nc.scalar.copy(bc_parts[FIRST:P, chunk[c]], psum[FIRST:P, c % 2, :]).then_inc(M["bc1_ready"], 1)
                    nc.scalar.copy(bc_rest[SECOND:P, c, :], psum[SECOND:P, c % 2, :]).then_inc(M["bc_full_ready"], 1)

                def second(c):
                    act.wait_ge(M["bc_rest_ready"], c + 1)
                    nc.scalar.copy(bc_parts[SECOND:P, chunk[c]], bc_rest[SECOND:P, c, :]).then_inc(M["bc2_ready"], 1)

                def magnitude(c):
                    act.wait_ge(M["v_psum"], c + 1)
                    nc.scalar.activation(soft_exp[:, c], v_banks[c], ACT.Abs).then_inc(M["soft_abs_ready"], 1)

                def exponential(c):
                    act.wait_ge(M["soft_abs_ready"], c + 1)
                    nc.scalar.activation(soft_exp[:, c], soft_exp[:, c], ACT.Exp, scale=-1.0
                                         ).then_inc(M["soft_exp_ready"], 1)

                def logarithm(c):
                    act.wait_ge(M["soft_exp_ready"], c + 1)
                    nc.scalar.activation(dt[:, :, chunk[c]], soft_exp[:, c], ACT.Ln, bias=1.0
                                         ).then_inc(M["soft_ln_ready"], 1)

                hold(0)
                hold(1)
                silu_gate(0)
                hold(2)
                silu_gate(1)
                silu_conv(0)
                hold(3)
                silu_gate(2)
                ranks(0)
                silu_conv(1)
                silu_gate(3)
                magnitude(0)
                ranks(1)
                silu_conv(2)
                magnitude(1)
                silu_conv(3)
                nc.scalar.preload_act_table_set("natural_log_exp_and_others")
                exponential(0)
                logarithm(0)
                ranks(2)
                exponential(1)
                ranks(3)
                logarithm(1)
                second(0)
                second(1)
                magnitude(2)
                exponential(2)
                magnitude(3)
                exponential(3)
                logarithm(2)
                logarithm(3)
                second(2)
                second(3)
                nc.scalar.activation(A_sb[:], A_sb[:], ACT.Exp).then_inc(M["A_exp"], 1)

            @block.tensor
            def _(pe):
                pe.wait_ge(loaded_m, 16 * M_LOADS)
                norm_transposes(pe, M["norm"], NG)

                def inner(c, z):
                    wait_xnT(pe, M["norm"], c)
                    if z:
                        wait_xnT(pe, M["norm"], NG // 2 + 1)
                        wait_xnT(pe, M["norm"], NG // 2)
                    if c >= 2:
                        pe.wait_ge(M["silu_z_ready"] if z else M["xc_pre_ready"], c - 1)
                    for h in range(NH):
                        m = z * NH + h
                        mm = nc.tensor.matmul(psum[:, z * NG + 2 * (c % 2) + h, :], W_in_sb[:, m * P:(m + 1) * P],
                                              xnT[:, chunk[c]], start=True, stop=True)
                    mm.then_inc(M["z_psum"] if z else M["xc_psum"], 1)

                inner(0, 0)
                inner(1, 0)
                for c in range(NC):
                    inner(c, 1)
                    if c + 2 < NC:
                        inner(c + 2, 0)

                def project(c):
                    pe.wait_ge(M["xc_ready"], NH * (c + 1))
                    if c < 2:
                        pe.wait_ge(M["xc_pre_ready"], 3 + c)
                    else:
                        pe.wait_ge(M["bc_full_ready"], c - 1)
                    for h in range(NH):
                        mm = nc.tensor.matmul(psum[:, c % 2, :], W_x_sb[:, h, :], xc[:, h, chunk[c]],
                                              start=(h == 0), stop=(h == NH - 1))
                    mm.then_inc(M["proj_psum"], 1)

                def delta(c):
                    pe.wait_ge(M["dtr_ready"], c + 1)
                    pe.wait_ge(M["pads_clear"], 1)
                    if c == 0:
                        pe.wait_ge(M["xc_pre_ready"], NC)
                    elif c < NC - 1:
                        pe.wait_ge(M["silu_z_ready"], c + 2)
                    else:
                        pe.wait_ge(M["bc_full_ready"], NC)
                    for h in range(NH):
                        mm = nc.tensor.matmul(v_banks[c][:, h, :], W_dt_sb[:, h * P:(h + 1) * P],
                                              dt_rank[:, c % 2, :], start=True, stop=True)
                    mm.then_inc(M["v_psum"], 1)

                project(0)
                delta(0)
                project(1)
                delta(1)
                project(2)
                project(3)
                delta(2)
                delta(3)

        with nc.Block() as block:
            dA_bank = [psum[:, h, :] for h in range(NH)]
            C_bank = [psum[:, 2 + k, :] for k in range(2)]
            B_bank = psum[:, 4, :]
            y_bank = [psum[:, 5 + h, :] for h in range(NH)]
            y_banks = psum[:, 5:5 + NH, :]
            o_bank = psum[:, 7, :]
            POOL_GROUP = NG - 1

            def scale_rows(engine, g, done):
                rows = xn_tok[:, g * GROUP * D:(g + 1) * GROUP * D].rearrange("p (j d) -> p j d", d=D)
                engine.tensor_tensor(rows, rows, ln_g_sb[:].unsqueeze(1).broadcast_to([P, GROUP, D]),
                                     ALU.mult).then_inc(done, 1)

            def add_rows(engine, g, done):
                rows = slice(g * GROUP * D, (g + 1) * GROUP * D)
                engine.tensor_tensor(x_tok[:, rows], x_tok[:, rows], xn_tok[:, rows], ALU.add).then_inc(done, 1)

            @block.sync
            def _(sp):
                pass

            @block.gpsimd
            def _(pool):
                def step(k, c, parity):
                    pool.wait_ge(M["B_ready"], k + 1)
                    pool.wait_ge(M["scan_done"][NH - 1], k + 1)
                    nc.gpsimd.tensor_tensor(dBx[:, parity], dtx[:, :, chunk[c]],
                                            B_sb[:, parity:parity + 1, :].broadcast_to([P, NH, CH]),
                                            ALU.mult).then_inc(M["dBx_ready"], 1)

                for c in range(NC):
                    with pool.Fori(0, S // SLOTS) as i:
                        for q in range(SLOTS):
                            step(c * S + SLOTS * i + q, c, q % 2)
                pool.wait_ge(M["out_norm"]["xn_even"], GROUP // 2 * (POOL_GROUP + 1))
                pool.wait_ge(M["out_norm"]["xn_odd"], GROUP // 2 * (POOL_GROUP + 1))
                scale_rows(nc.gpsimd, POOL_GROUP, M["scale_ready_pool"])
                pool.wait_ge(M["scale_ready_pool"], 1)
                add_rows(nc.gpsimd, POOL_GROUP, M["x_ready_pool"])
                pool.wait_ge(M["x_ready_pool"], 1)

            @block.vector
            def _(dve):
                for h in range(NH):
                    nc.vector.sem_inc(M["scan_done"][h], 2)

                def scans(k, s, slot):
                    for h in range(NH):
                        dve.wait_ge(M["dA_ready"][h], k + 1)
                        nc.vector.tensor_tensor_scan(H[:, slot, h, :], dA_bank[h], dBx[:, slot % 2, h, :],
                                                     carry[:, ds(s * NH + h, 1)],
                                                     ALU.mult, ALU.add).then_inc(M["scan_done"][h], 1)

                def product(k, slot):
                    dve.wait_ge(M["C_psum"], k + 1)
                    nc.vector.tensor_tensor(hC[:, slot % 2], H[:, slot],
                                            C_bank[slot % 2].unsqueeze(1).broadcast_to([P, NH, CH]),
                                            ALU.mult).then_inc(M["hC_ready"], 1)

                def gate(c, y, y_ready, count):
                    dve.wait_ge(y_ready, count)
                    if c >= 1:
                        dve.wait_ge(M["o_psum"], c * GROUP)
                    nc.vector.tensor_tensor(yz, y, silu_z[:, :, chunk[c]], ALU.mult).then_inc(M["yz_ready"], 1)

                for c in range(NC):
                    first = c * S
                    if c % CPB == 0:
                        if c >= 1:
                            dve.wait_ge(M["carry_ready"], first)
                        nc.vector.memset(carry[:], 0.0).then_inc(M["carry_clear"], 1)
                        dve.wait_ge(M["carry_clear"], c // CPB + 1)
                    for s in range(SLOTS):
                        scans(first + s, s, s)
                        if first + s >= 1:
                            product(first + s - 1, (s - 1) % SLOTS)
                    if c >= 1:
                        gate(c - 1, y_sb, M["y_ready"], c)
                    with dve.Fori(1, S // SLOTS) as i:
                        for slot in range(SLOTS):
                            s = SLOTS * i + slot
                            scans(first + s, s, slot)
                            product(first + s - 1, (slot - 1) % SLOTS)
                dve.wait_ge(M["scan_done"][NH - 1], NC * S + 2)
                product(NC * S - 1, SLOTS - 1)
                gate(NC - 1, y_banks, M["sum_done"], NC)
                norm_vector(dve, M["out_norm"], y_tok, arrives=(M["o_ready"], 1))
                dve.wait_ge(M["x_plus_b"], 2)
                for g in range(POOL_GROUP):
                    dve.wait_ge(M["out_norm"]["xn_even"], GROUP // 2 * (g + 1))
                    dve.wait_ge(M["out_norm"]["xn_odd"], GROUP // 2 * (g + 1))
                    scale_rows(nc.vector, g, M["scale_ready"])
                for g in range(POOL_GROUP):
                    dve.wait_ge(M["scale_ready"], g + 1)
                    add_rows(nc.vector, g, M["x_ready"])
                dve.wait_ge(M["x_ready"], POOL_GROUP)

            @block.scalar
            def _(act):
                def spread(k, parity):
                    act.wait_ge(M["B_psum"], k + 1)
                    nc.scalar.copy(B_sb[:, parity, :], B_bank).then_inc(M["B_ready"], 1)

                def decay(k, c, s):
                    act.wait_ge(M["dBx_ready"], k + 1)
                    for h in range(NH):
                        act.wait_ge(M["scan_done"][h], k + 2)
                        nc.scalar.activation(dA_bank[h], dt[:, h, chunk[c]], ACT.Exp,
                                             scale=neg_A[:, ds(s + h * S, 1)]).then_inc(M["dA_ready"][h], 1)

                def keep(k, s, slot):
                    act.wait_ge(M["scan_done"][NH - 1], k + 3)
                    nc.scalar.copy(carry[:, ds(s * NH, NH)], H[:, slot, :, CH - 1]).then_inc(M["carry_ready"], 1)

                def leave(c):
                    act.wait_ge(M["sum_done"], c + 1)
                    if c >= 1:
                        act.wait_ge(M["yz_ready"], c)
                    nc.scalar.copy(y_sb, y_banks).then_inc(M["y_ready"], 1)

                def rows_out(c):
                    act.wait_ge(M["o_psum"], (c + 1) * GROUP)
                    nc.scalar.copy(y_tok[:, c * GROUP * D:(c + 1) * GROUP * D], o_bank).then_inc(M["o_ready"], 1)

                spread(0, 0)
                spread(1, 1)
                for c in range(NC):
                    first = c * S
                    for s in range(SLOTS):
                        decay(first + s, c, s)
                        if first + s >= 1:
                            keep(first + s - 1, (s - 1) % S, (s - 1) % SLOTS)
                        spread(first + s + 2, s % 2)
                        if s == 1 and c >= 1:
                            leave(c - 1)
                    with act.Fori(1, S // SLOTS) as i:
                        for slot in range(SLOTS):
                            s = SLOTS * i + slot
                            decay(first + s, c, s)
                            keep(first + s - 1, s - 1, (slot - 1) % SLOTS)
                            spread(first + s + 2, slot % 2)
                    if c >= 1:
                        rows_out(c - 1)
                rows_out(NC - 1)
                norm_scalar(act, M["out_norm"], y_tok)

            @block.tensor
            def _(pe):
                def spread(bank, row, c, done):
                    nc.tensor.matmul(bank, pick_row[:, ds(row, 1)].broadcast_to([P, P]),
                                     bc_parts[:, c * CH:(c + 1) * CH], start=True, stop=True).then_inc(done, 1)

                def step(k, parity, C_next, B_next, c=0, first=False, last=False):
                    if B_next is not None:
                        pe.wait_ge(M["B_ready"], k + 4)
                        spread(B_bank, B_next[1], B_next[0], M["B_psum"])
                    pe.wait_ge(M["hC_ready"], k + 1)
                    if first:
                        if c >= 1:
                            pe.wait_ge(M["y_ready"], c)
                        for h in range(NH):
                            nc.tensor.matmul(y_bank[h], D_diag[:, h, :], xc[:, h, chunk[c]], start=True, stop=False)
                    for h in range(NH):
                        mm = nc.tensor.matmul(y_bank[h], ident[:], hC[:, parity, h, :], start=False, stop=last)
                    if last:
                        mm.then_inc(M["sum_done"], 1)
                    spread(C_bank[parity], S + C_next[1], C_next[0], M["C_psum"])

                def project(c):
                    pe.wait_ge(M["yz_ready"], c + 1)
                    if c >= 1:
                        pe.wait_ge(M["o_ready"], c)
                    for t in range(GROUP):
                        for h in range(NH):
                            mm = nc.tensor.matmul(o_bank[:, t * D:(t + 1) * D], yz[:, h, t * P:(t + 1) * P],
                                                  W_out_sb[:, h, :], start=(h == 0), stop=(h == NH - 1))
                        mm.then_inc(M["o_psum"], 1)

                spread(B_bank, 0, 0, M["B_psum"])
                spread(C_bank[0], S, 0, M["C_psum"])
                spread(C_bank[1], S + 1, 0, M["C_psum"])
                for n in (1, 2, 3):
                    pe.wait_ge(M["B_ready"], n)
                    spread(B_bank, n, 0, M["B_psum"])
                AHEAD = 4
                for c in range(NC):
                    k = c * S
                    for s in range(AHEAD):
                        step(k + s, s % 2, (c, s + 2), (c, s + 4), c, first=(s == 0))
                    with pe.Fori(1, S // AHEAD - 1) as i:
                        for q in range(AHEAD):
                            s = AHEAD * i + q
                            step(k + s, q % 2, (c, s + 2), (c, s + 4))
                    if c >= 1:
                        project(c - 1)
                    for s in range(S - AHEAD, S):
                        spread_ahead = k + s + 4 < NC * S + 2
                        step(k + s, s % 2, (c + (s + 2) // S, (s + 2) % S),
                             (c + 1, s + 4 - S) if spread_ahead else None, last=(s == S - 1))
                project(NC - 1)

        with nc.Block() as block:
            @block.sync
            def _(sp):
                ffn_sync(sp, FF[1])
                sp.wait_ge(FF[1]["combined"], NT)
                sp.dma_start(out.rearrange("b (j p) d -> p (b j) d", p=P),
                             x_tok[:].rearrange("p (j d) -> p j d", d=D)).then_inc(out_stored, 16)
                sp.wait_ge(out_stored, 16)

            @block.gpsimd
            def _(pool):
                ffn_gpsimd(pool, FF[1])

            @block.vector
            def _(dve):
                ffn_vector(dve, FF[1])

            @block.scalar
            def _(act):
                ffn_scalar(act, FF[1])

            @block.tensor
            def _(pe):
                ffn_tensor(pe, FF[1])


_NAMES = ["attn_x", "attn_W_in", "attn_conv_w", "attn_conv_b", "attn_W_x", "attn_W_dt", "attn_b_dt", "attn_A_log",
          "attn_D_skip", "attn_W_out", "attn_ln_g", "attn_ln_b", "ffn_router_w", "ffn_router_b", "ffn_w1", "ffn_w2"]


def kernel(**inputs):
    import numpy as np
    import concourse.bacc as bacc
    from concourse.bass_utils import run_bass_kernel_spmd

    nc = bacc.Bacc("TRN2", target_bir_lowering=False, num_devices=1)
    arrays, args = {}, []
    for name in _NAMES:
        a = np.ascontiguousarray(inputs["L0_" + name])
        arrays[name] = a
        args.append(nc.dram_tensor(name, a.shape, mybir.dt.from_np(a.dtype), kind="ExternalInput").ap())
    shape = inputs["L0_attn_x"].shape
    args.append(nc.dram_tensor("out", shape, F32, kind="ExternalOutput").ap())
    macaron_kernel(nc, *args)
    r = run_bass_kernel_spmd(nc, [arrays], core_ids=[0])
    return r.results[0]["out"]
```

```python
from contextlib import ExitStack

import concourse.bass as bass
from concourse import mybir

ALU = mybir.AluOpType
ACT = mybir.ActivationFunctionType
AX = mybir.AxisListType
F32 = mybir.dt.float32
BF16 = mybir.dt.bfloat16
I32 = mybir.dt.int32
U32 = mybir.dt.uint32

P = 128
EPS = 1e-5
GROUP = 4


def macaron_kernel(nc, x_in, W_in, conv_w, conv_b, W_x, W_dt, b_dt, A_log, D_skip, W_out, ln_g, ln_b,
                   router_w, router_b, w1, w2, out):
    B, L, D = x_in.shape
    N = B * L
    NT = N // P
    NG = NT // GROUP
    E = router_w.shape[1]
    F = w2.shape[1]
    FC = F // P
    DI = W_out.shape[0]
    NH = DI // P
    S = A_log.shape[1]
    TAPS = conv_w.shape[1]
    R = W_dt.shape[0]
    FIRST, SECOND, THIRD = R, R + 2 * S, R - 2 * S
    assert SECOND + 2 * S == P and THIRD % 32 == 0
    CH = 512
    NC = N // CH
    CPB = L // CH
    SLOT_TILES = (N + E * (P - 1)) // P
    PAD = TAPS - 1
    LOG_P = P.bit_length() - 1
    M_LOADS = 10 + 2 * NH
    ds = bass.ds
    assert D == P and NH == 2 and E == 8 and 2 * S == 32 and SLOT_TILES % 2 == 1

    with ExitStack() as ctx:
        def sb(name, shape, dt=F32):
            return ctx.enter_context(nc.sbuf_tensor(name, shape, dt))

        def sem(name):
            return ctx.enter_context(nc.semaphore(name))

        xn_rows = nc.dram_tensor("xn_rows", (N, D), F32).ap()
        y_rows = nc.dram_tensor("y_rows", (N + SLOT_TILES * P, D), F32).ap()

        ident = sb("ident", [P, P])
        earlier = sb("earlier", [P, P], BF16)
        ones = sb("ones", [P, P], BF16)
        expert_iota_i = sb("expert_iota_i", [P, NT, E], I32)
        expert_iota = sb("expert_iota", [P, NT, E])
        tile_iota_i = sb("tile_iota_i", [P, SLOT_TILES], I32)
        tile_iota = sb("tile_iota", [P, SLOT_TILES])
        lane_iota = sb("lane_iota", [P, P], I32)
        token_tile_i = sb("token_tile_i", [P, NT], I32)
        token_tile = sb("token_tile", [P, NT])
        partition_i = sb("partition_i", [P, 1], I32)
        partition = sb("partition", [P, 1])
        spare_row_i = sb("spare_row_i", [P, SLOT_TILES], I32)
        spare_row = sb("spare_row", [P, SLOT_TILES])
        scan_keep = sb("scan_keep", [P, E, NT])
        ones_e = sb("ones_e", [P, E])
        pick_row = sb("pick_row", [P, 2 * S], BF16)

        w1_sb = sb("w1_sb", [P, E * 2 * F])
        w2_sb = sb("w2_sb", [P, E * FC * D])
        router_sb = sb("router_sb", [P, E])
        router_b_sb = sb("router_b_sb", [P, E])
        W_in_sb = sb("W_in_sb", [P, 2 * DI])
        W_x_sb = sb("W_x_sb", [P, NH, P])
        W_dt_sb = sb("W_dt_sb", [R + 1, DI])
        W_out_sb = sb("W_out_sb", [P, NH, D])
        conv_w_sb = sb("conv_w_sb", [P, NH, TAPS])
        conv_b_sb = sb("conv_b_sb", [P, NH])
        D_skip_sb = sb("D_skip_sb", [P, NH])
        D_diag = sb("D_diag", [P, NH, P])
        A_sb = sb("A_sb", [P, NH, S])
        neg_A = sb("neg_A", [P, NH * S])
        ln_g_sb = sb("ln_g_sb", [P, D])
        ln_b_sb = sb("ln_b_sb", [P, D])

        x_tok = sb("x_tok", [P, NT * D])
        xn_tok = sb("xn_tok", [P, NT * D])
        xnT = sb("xnT", [P, N])
        y_tok = xnT

        stats = sb("stats", [P, NT, 6])
        mean = sb("mean", [P, NT])
        mean_diff = sb("mean_diff", [P, NT])
        var = sb("var", [P, NT])
        std = sb("std", [P, NT])
        rstd_try = sb("rstd_try", [P, NT])
        rstd_fix = sb("rstd_fix", [P, NT])
        rstd = sb("rstd", [P, NT])
        shift = sb("shift", [P, NT])

        logits = sb("logits", [P, NT, E])
        top_logit = sb("top_logit", [P, NT])
        expo = sb("expo", [P, NT, E])
        expo_sum = sb("expo_sum", [P, NT])
        half_prob = sb("half_prob", [P, NT])
        below_top = sb("below_top", [P, NT, E])
        first_top = sb("first_top", [P, NT])
        chosen = sb("chosen", [P, E, NT], BF16)
        upto_tile = sb("upto_tile", [P, E * NT])
        expert_tiles_i = sb("expert_tiles_i", [P, E], I32)
        expert_tiles = sb("expert_tiles", [P, E])
        last_tile = sb("last_tile", [P, E])
        first_tile = sb("first_tile", [P, E])
        slot_of = sb("slot_of", [P, E, NT])
        slot_f = sb("slot_f", [P, NT])
        slot = sb("slot", [P, NT], I32)
        slot_tile = sb("slot_tile", [P, NT], I32)
        slot_lane = sb("slot_lane", [P, NT], I32)
        slot_info = sb("slot_info", [P, 3, SLOT_TILES])
        slot_token = sb("slot_token", [P, SLOT_TILES])
        spare = sb("spare", [P, SLOT_TILES])
        gather_row = sb("gather_row", [P, SLOT_TILES], U32)
        scatter_row = sb("scatter_row", [P, SLOT_TILES], U32)
        tile_past = sb("tile_past", [1, SLOT_TILES, E])
        tile_expert_f = sb("tile_expert_f", [1, SLOT_TILES])
        tile_expert = sb("tile_expert", [1, SLOT_TILES], I32)

        SLOTS = 4
        phase = sb("phase", [P, NH * B * (PAD + L) + 16 * CH])

        def carve(*shapes):
            views, at = [], 0
            for rows, *dims in shapes:
                size = 1
                for n in dims:
                    size *= n
                flat = phase[0:rows, at:at + size]
                names = "abc"[:len(dims)]
                if len(dims) > 1:
                    flat = flat.rearrange(f"p ({' '.join(names)}) -> p {' '.join(names)}", **dict(zip(names, dims)))
                views.append(flat)
                at += size
            assert at <= phase.shape[1]
            return views

        xs_sb, xsT_sb, w1_tile, gate_sb, u_sb, ys_sb, lanes, tiles3 = carve(
            (P, 2, D), (P, 2, P), (P, 2, 2 * F), (P, 2, F), (P, 2, F), (P, 2, D), (P, NT * P // 2),
            (P, NT * 3 * SLOT_TILES // 2))
        at_lane = lanes.bitcast(BF16).rearrange("p (j m) -> p j m", m=P)
        at_tile = tiles3.bitcast(BF16).rearrange("p (j a t) -> p j a t", a=3, t=SLOT_TILES)
        xc_pre, dt_rank, soft_exp, bc_rest = carve(
            (P, NH, B, PAD + L), (R + 1, 2, CH), (P, NC, NH, CH), (P, NC, CH))
        B_sb, dBx, H, hC, yz = carve(
            (P, 2, CH), (P, 2, NH, CH), (P, SLOTS, NH, CH), (P, 2, NH, CH), (P, NH, CH))

        xc = sb("xc", [P, NH, N])
        silu_z = sb("silu_z", [P, NH, N])
        dt = sb("dt", [P, NH, N])
        dtx = sb("dtx", [P, NH, N])
        carry = sb("carry", [P, S * NH])
        bc_parts = sb("bc_parts", [P, N + CH], BF16)

        psum = ctx.enter_context(nc.psum_tensor("psum", [P, 8, 512], F32))

        loaded_x = sem("loaded_x")
        loaded_small = sem("loaded_small")
        loaded_w = sem("loaded_w")
        loaded_m = sem("loaded_m")
        ident_ready = sem("ident_ready")
        consts_ready = sem("consts_ready")
        pool_step = sem("pool_step")
        dve_step = sem("dve_step")
        out_stored = sem("out_stored")
        pool_count, dve_count = [0], [0]

        def norm_sems(tag):
            return {n: sem(f"{tag}_{n}") for n in (
                "stats_done", "var_ready", "std_ready", "shift_ready", "xn_even", "xn_odd", "xnT_psum", "xnT_even",
                "xnT_odd")}

        def ffn_sems(tag):
            f = {n: sem(f"{tag}_{n}") for n in (
                "logits_psum", "sub_ready", "expo_ready", "chosen_ready", "prefix_psum", "at_tile_ready",
                "at_lane_ready", "info_psum", "gather_row_ready", "scatter_row_ready", "tile_expert_ready", "xn_stored",
                "xsT_psum", "xsT_ready", "w1_ready", "h_a", "h_g", "gate_ready", "u_ready", "ys_psum",
                "ys_ready", "combined")}
            f["y_loaded"] = [sem(f"{tag}_y_loaded{g}") for g in range(NG)]
            f["xs_loaded"] = [sem(f"{tag}_xs_loaded{k}") for k in range(2)]
            f["ys_stored"] = [sem(f"{tag}_ys_stored{k}") for k in range(2)]
            f["norm"] = norm_sems(tag)
            return f

        FF = [ffn_sems("ffn0"), ffn_sems("ffn1")]
        M = {n: sem(f"m_{n}") for n in (
            "A_exp", "neg_A_ready", "pads_clear", "pick_ready", "xc_psum", "z_psum", "xc_pre_ready", "silu_z_ready",
            "conv_step", "xc_ready", "proj_psum", "dtr_ready", "v_psum", "soft_abs_ready", "soft_exp_ready",
            "soft_ln_ready", "round_ready", "err_ready", "log_ready", "dve_err_ready", "dve_log_ready", "dt_ready",
            "dtx_ready", "bc1_ready", "bc_full_ready", "bc_rest_ready", "bc2_ready", "bc3_ready", "x_plus_b",
            "B_psum", "B_ready", "C_psum", "dBx_ready", "hC_ready", "sum_done", "carry_clear", "carry_ready",
            "yz_ready", "o_psum", "o_ready", "scale_ready", "x_ready", "scale_ready_pool", "x_ready_pool")}
        M["scan_done"] = [sem(f"m_scan_done{h}") for h in range(NH)]
        M["dA_ready"] = [sem(f"m_dA_ready{h}") for h in range(NH)]
        M["norm"] = norm_sems("m")
        M["out_norm"] = norm_sems("mo")

        def norm_statistics(dve, s, src, arrives):
            for j in range(NT):
                if arrives and j % GROUP == 0:
                    signal, by_group = arrives
                    dve.wait_ge(signal, by_group * (j // GROUP + 1))
                last = nc.vector.bn_stats(stats[:, j, :], src[:, j * D:(j + 1) * D])
            last.then_inc(s["stats_done"], 1)
            dve.wait_ge(s["stats_done"], 1)
            mean_even, mean_odd = stats[:, :, 1], stats[:, :, 4]
            nc.vector.tensor_tensor(mean_diff[:], mean_even, mean_odd, ALU.subtract)
            nc.vector.tensor_tensor(mean[:], mean_even, mean_odd, ALU.add)
            chain(dve, nc.vector.tensor_tensor(var[:], stats[:, :, 2], stats[:, :, 5], ALU.add))
            nc.vector.tensor_scalar(mean[:], mean[:], 0.5, None, ALU.mult)
            nc.vector.tensor_scalar(var[:], var[:], 1.0 / D, EPS, ALU.mult, ALU.add)
            chain(dve, nc.vector.scalar_tensor_tensor(out=mean_diff[:], in0=mean_diff[:], scalar=0.25,
                                                      in1=mean_diff[:], op0=ALU.mult, op1=ALU.mult))
            nc.vector.tensor_tensor(var[:], var[:], mean_diff[:], ALU.add).then_inc(s["var_ready"], 1)
            dve.wait_ge(s["std_ready"], 1)
            chain(dve, nc.vector.reciprocal(rstd_try[:], std[:]))
            chain(dve, nc.vector.scalar_tensor_tensor(out=rstd_fix[:], in0=rstd_try[:], scalar=-0.5, in1=rstd_try[:],
                                                      op0=ALU.mult, op1=ALU.mult))
            chain(dve, nc.vector.tensor_tensor(rstd_fix[:], rstd_fix[:], var[:], ALU.mult))
            chain(dve, nc.vector.scalar_tensor_tensor(out=rstd[:], in0=rstd_fix[:], scalar=1.5, in1=rstd_try[:],
                                                      op0=ALU.add, op1=ALU.mult))
            nc.vector.scalar_tensor_tensor(out=shift[:], in0=mean[:], scalar=-1.0, in1=rstd[:], op0=ALU.mult,
                                           op1=ALU.mult).then_inc(s["shift_ready"], 1)

        def norm_vector(dve, s, src, arrives=None):
            norm_statistics(dve, s, src, arrives)
            for j in range(0, NT, 2):
                nc.vector.tensor_scalar(xn_tok[:, j * D:(j + 1) * D], src[:, j * D:(j + 1) * D], mean[:, j:j + 1],
                                        rstd[:, j:j + 1], ALU.subtract, ALU.mult).then_inc(s["xn_even"], 1)

        def norm_scalar(act, s, src, next_function=None):
            nc.scalar.preload_act_table(ACT.Sqrt)
            act.wait_ge(s["var_ready"], 1)
            nc.scalar.activation(std[:], var[:], ACT.Sqrt).then_inc(s["std_ready"], 1)
            if next_function is not None:
                nc.scalar.preload_act_table(next_function)
            act.wait_ge(s["shift_ready"], 1)
            for j in range(1, NT, 2):
                nc.scalar.activation(xn_tok[:, j * D:(j + 1) * D], src[:, j * D:(j + 1) * D], ACT.Identity,
                                     bias=shift[:, j:j + 1], scale=rstd[:, j:j + 1]).then_inc(s["xn_odd"], 1)

        def chain(dve, instruction):
            dve_count[0] += 1
            instruction.then_inc(dve_step, 1)
            dve.wait_ge(dve_step, dve_count[0])

        def keep_warm(count, bank):
            for _ in range(count):
                nc.tensor.matmul(psum[:, bank, 0:P], ident[:], ident[:], start=True, stop=True)

        def norm_transposes(pe, s, bank):
            for g in range(NG):
                pe.wait_ge(s["xn_even"], GROUP // 2 * (g + 1))
                pe.wait_ge(s["xn_odd"], GROUP // 2 * (g + 1))
                for k in range(GROUP):
                    j = g * GROUP + k
                    nc.tensor.transpose(psum[:, bank + g, k * P:(k + 1) * P], xn_tok[:, j * D:(j + 1) * D],
                                        ident[:]).then_inc(s["xnT_psum"], 1)

        def pool_chain(pool, instruction):
            pool_count[0] += 1
            instruction.then_inc(pool_step, 1)
            pool.wait_ge(pool_step, pool_count[0])

        def wait_xnT(pe, s, g):
            pe.wait_ge(s["xnT_odd" if g % 2 else "xnT_even"], g // 2 + 1)

        def norm_evacuate(engine, copy, s, bank, groups, done):
            for g in groups:
                engine.wait_ge(s["xnT_psum"], GROUP * (g + 1))
                copy(xnT[:, g * CH:(g + 1) * CH], psum[:, bank + g, :]).then_inc(done, 1)

        def ffn_sync(sp, f):
            by_token = "(j p) d -> p j d"
            for g in range(NG):
                sp.wait_ge(f["norm"]["xn_even"], GROUP // 2 * (g + 1))
                sp.wait_ge(f["norm"]["xn_odd"], GROUP // 2 * (g + 1))
                sp.dma_start(xn_rows[g * CH:(g + 1) * CH, :].rearrange(by_token, p=P),
                             xn_tok[:, g * GROUP * D:(g + 1) * GROUP * D].rearrange("p (j d) -> p j d", d=D)
                             ).then_inc(f["xn_stored"], 16)
            sp.wait_ge(f["ys_stored"][0], 16 * (SLOT_TILES // 2 + 1))
            sp.wait_ge(f["ys_stored"][1], 16 * (SLOT_TILES // 2))
            for g in range(NG):
                sp.dma_start(y_tok[:, g * GROUP * D:(g + 1) * GROUP * D].rearrange("p (j d) -> p j d", d=D),
                             y_rows[g * CH:(g + 1) * CH, :].rearrange(by_token, p=P)).then_inc(f["y_loaded"][g], 16)

        def ffn_gpsimd(pool, f):
            def gather(t):
                if t >= 2:
                    pool.wait_ge(f["xsT_psum"], t - 1)
                nc.gpsimd.indirect_dma_start(xs_sb[:, t % 2, :], None, xn_rows,
                                             bass.IndirectOffsetOnAxis(ap=gather_row[:, t:t + 1], axis=0)
                                             ).then_inc(f["xs_loaded"][t % 2], 16)

            def scatter(t):
                pool.wait_ge(f["ys_ready"], t + 1)
                nc.gpsimd.indirect_dma_start(y_rows, bass.IndirectOffsetOnAxis(ap=scatter_row[:, t:t + 1], axis=0),
                                             ys_sb[:, t % 2, :], None).then_inc(f["ys_stored"][t % 2], 16)

            pool.wait_ge(f["xn_stored"], 16 * NG)
            pool.wait_ge(f["gather_row_ready"], 1)
            for t in range(4):
                gather(t)
            pool.wait_ge(f["scatter_row_ready"], 1)
            for t in range(SLOT_TILES):
                if t + 4 < SLOT_TILES:
                    gather(t + 4)
                scatter(t)

        def ffn_vector(dve, f):
            norm_vector(dve, f["norm"], x_tok)
            norm_evacuate(dve, nc.vector.tensor_copy, f["norm"], 0, range(0, NG, 2), f["norm"]["xnT_even"])
            dve.wait_ge(loaded_small, 32)
            dve.wait_ge(consts_ready, 1)
            dve.wait_ge(f["logits_psum"], NT)
            router_bias = router_b_sb[:].unsqueeze(1).broadcast_to([P, NT, E])
            top = top_logit[:].unsqueeze(2).broadcast_to([P, NT, E])
            chain(dve, nc.vector.tensor_tensor(logits[:], psum[:, 4, 0:NT * E].rearrange("p (j e) -> p j e", e=E),
                                               router_bias, ALU.add))
            chain(dve, nc.vector.tensor_reduce(top_logit[:], logits[:], AX.X, ALU.max))
            chain(dve, nc.vector.tensor_tensor(below_top[:], logits[:], top, ALU.is_lt))
            chain(dve, nc.vector.scalar_tensor_tensor(out=below_top[:], in0=below_top[:], scalar=float(E),
                                                      in1=expert_iota[:], op0=ALU.mult, op1=ALU.add))
            chain(dve, nc.vector.tensor_reduce(first_top[:], below_top[:], AX.X, ALU.min))
            nc.vector.tensor_tensor(chosen[:].rearrange("p e j -> p j e"), below_top[:],
                                    first_top[:].unsqueeze(2).broadcast_to([P, NT, E]),
                                    ALU.is_equal).then_inc(f["chosen_ready"], 1)
            nc.vector.tensor_tensor(logits[:], logits[:], top, ALU.subtract).then_inc(f["sub_ready"], 1)
            dve.wait_ge(f["prefix_psum"], 2)
            in_tile, of_tile = psum[:, 5, 0:E * NT], psum[:, 6, 0:E * NT]
            chain(dve, nc.vector.tensor_tensor_scan(upto_tile[:], scan_keep[:].rearrange("p e j -> p (e j)"),
                                                    of_tile, 0.0, ALU.mult, ALU.add))
            counts = upto_tile[:].rearrange("p (e j) -> p e j", e=E)[:, :, NT - 1]
            chain(dve, nc.vector.tensor_scalar(expert_tiles_i[:], counts, float(P - 1), None, ALU.add))
            nc.vector.tensor_tensor(upto_tile[:], upto_tile[:], of_tile, ALU.subtract)
            chain(dve, nc.vector.tensor_scalar(expert_tiles_i[:], expert_tiles_i[:], LOG_P, None, ALU.arith_shift_right))
            nc.vector.tensor_copy(expert_tiles[:], expert_tiles_i[:])
            chain(dve, nc.vector.tensor_tensor(upto_tile[:], upto_tile[:], in_tile, ALU.add))
            chain(dve, nc.vector.tensor_tensor_scan(last_tile[:], ones_e[:], expert_tiles[:], 0.0, ALU.mult, ALU.add))
            chain(dve, nc.vector.tensor_tensor(first_tile[:], last_tile[:], expert_tiles[:], ALU.subtract))
            chain(dve, nc.vector.scalar_tensor_tensor(
                out=slot_of[:], in0=first_tile[:].unsqueeze(2).broadcast_to([P, E, NT]), scalar=float(P),
                in1=upto_tile[:].rearrange("p (e j) -> p e j", e=E), op0=ALU.mult, op1=ALU.add))
            chain(dve, nc.vector.tensor_tensor(slot_of[:], slot_of[:], chosen[:], ALU.mult))
            chain(dve, nc.vector.tensor_reduce(slot_f[:], slot_of[:].rearrange("p e j -> p j e"), AX.X, ALU.add))
            chain(dve, nc.vector.tensor_copy(slot[:], slot_f[:]))
            nc.vector.tensor_scalar(slot_tile[:], slot[:], LOG_P, None, ALU.arith_shift_right)
            chain(dve, nc.vector.tensor_scalar(slot_lane[:], slot[:], P - 1, None, ALU.bitwise_and))
            chain(dve, nc.vector.tensor_tensor(
                at_tile[:, :, 0, :], slot_tile[:].unsqueeze(2).broadcast_to([P, NT, SLOT_TILES]),
                tile_iota_i[:].unsqueeze(1).broadcast_to([P, NT, SLOT_TILES]), ALU.is_equal))
            nc.vector.tensor_scalar(at_tile[:, :, 1, :], at_tile[:, :, 0, :], partition[:], None, ALU.mult)
            nc.vector.tensor_tensor(at_tile[:, :, 2, :], at_tile[:, :, 0, :],
                                    token_tile[:].unsqueeze(2).broadcast_to([P, NT, SLOT_TILES]),
                                    ALU.mult).then_inc(f["at_tile_ready"], 1)
            for g in range(NG):
                tiles = slice(g * GROUP, (g + 1) * GROUP)
                nc.vector.tensor_tensor(at_lane[:, tiles, :],
                                        slot_lane[:, tiles].unsqueeze(2).broadcast_to([P, GROUP, P]),
                                        lane_iota[:].unsqueeze(1).broadcast_to([P, GROUP, P]),
                                        ALU.is_equal).then_inc(f["at_lane_ready"], 1)
            dve.wait_ge(f["info_psum"], 1)
            chain(dve, nc.vector.tensor_copy(slot_info[:].rearrange("p a t -> p (a t)"), psum[:, 7, 0:3 * SLOT_TILES]))
            nc.vector.scalar_tensor_tensor(out=gather_row[:], in0=slot_info[:, 2, :], scalar=float(P),
                                           in1=slot_info[:, 1, :], op0=ALU.mult, op1=ALU.add
                                           ).then_inc(f["gather_row_ready"], 1)
            chain(dve, nc.vector.tensor_tensor(
                tile_past[:], last_tile[0:1, :].unsqueeze(1).broadcast_to([1, SLOT_TILES, E]),
                tile_iota[0:1, :].unsqueeze(2).broadcast_to([1, SLOT_TILES, E]), ALU.is_le))
            chain(dve, nc.vector.tensor_reduce(tile_expert_f[:], tile_past[:], AX.X, ALU.add))
            nc.vector.tensor_scalar(tile_expert[:], tile_expert_f[:], float(E - 1), None,
                                    ALU.min).then_inc(f["tile_expert_ready"], 1)
            nc.vector.scalar_tensor_tensor(out=slot_token[:], in0=slot_info[:, 2, :], scalar=float(P),
                                           in1=slot_info[:, 1, :], op0=ALU.mult, op1=ALU.add)
            chain(dve, nc.vector.tensor_scalar(spare[:], slot_info[:, 0, :], -1.0, 1.0, ALU.mult, ALU.add))
            chain(dve, nc.vector.tensor_tensor(spare[:], spare[:], spare_row[:], ALU.mult))
            nc.vector.tensor_tensor(scatter_row[:], slot_token[:], spare[:], ALU.add).then_inc(f["scatter_row_ready"], 1)

            dve.wait_ge(f["expo_ready"], 1)
            chain(dve, nc.vector.tensor_reduce(expo_sum[:], expo[:], AX.X, ALU.add))
            chain(dve, nc.vector.reciprocal(half_prob[:], expo_sum[:]))
            chain(dve, nc.vector.tensor_scalar(half_prob[:], half_prob[:], 0.5, None, ALU.mult))

            def pick(t, k):
                e = nc.vector.value_load(tile_expert[0:1, ds(t, 1)], min_val=0, max_val=E - 1)
                if not isinstance(t, int) or t >= 2:
                    dve.wait_ge(f["h_g"], t - 1)
                nc.vector.tensor_copy(w1_tile[:, k, :], w1_sb[:, ds(e * (2 * F), 2 * F)]).then_inc(f["w1_ready"], 1)

            def gate(t, k):
                dve.wait_ge(f["gate_ready"], t + 1)
                dve.wait_ge(f["h_g"], t + 1)
                if not isinstance(t, int) or t >= 2:
                    dve.wait_ge(f["ys_psum"], t - 1)
                nc.vector.tensor_tensor(u_sb[:, k, :], gate_sb[:, k, :], psum[:, 2 * k + 1, :],
                                        ALU.mult).then_inc(f["u_ready"], 1)

            def step(t, k):
                pick(t + 1, 1 - k)
                gate(t, k)

            dve.wait_ge(f["tile_expert_ready"], 1)
            dve.wait_ge(loaded_w, 16 * 2 * E)
            pick(0, 0)
            step(0, 0)
            step(1, 1)
            with dve.Fori(1, (SLOT_TILES - 1) // 2) as i:
                step(2 * i, 0)
                step(2 * i + 1, 1)
            gate(SLOT_TILES - 1, 0)
            for g in range(NG):
                dve.wait_ge(f["y_loaded"][g], 16)
                for j in range(g * GROUP, (g + 1) * GROUP):
                    nc.vector.scalar_tensor_tensor(out=x_tok[:, j * D:(j + 1) * D], in0=y_tok[:, j * D:(j + 1) * D],
                                                   scalar=half_prob[:, j:j + 1], in1=x_tok[:, j * D:(j + 1) * D],
                                                   op0=ALU.mult, op1=ALU.add).then_inc(f["combined"], 1)
            dve.wait_ge(f["combined"], NT)

        def ffn_scalar(act, f):
            norm_scalar(act, f["norm"], x_tok, ACT.Exp)
            norm_evacuate(act, nc.scalar.copy, f["norm"], 0, range(1, NG, 2), f["norm"]["xnT_odd"])
            act.wait_ge(f["sub_ready"], 1)
            nc.scalar.activation(expo[:], logits[:], ACT.Exp).then_inc(f["expo_ready"], 1)
            nc.scalar.preload_act_table(ACT.Silu)

            def silu(t, k):
                act.wait_ge(f["h_a"], t + 1)
                if not isinstance(t, int) or t >= 2:
                    act.wait_ge(f["u_ready"], t - 1)
                nc.scalar.activation(gate_sb[:, k, :], psum[:, 2 * k, :], ACT.Silu).then_inc(f["gate_ready"], 1)

            def turn(t, k):
                act.wait_ge(f["xsT_psum"], t + 1)
                if not isinstance(t, int) or t >= 2:
                    act.wait_ge(f["h_g"], t - 1)
                nc.scalar.copy(xsT_sb[:, k, :], psum[:, 7, k * P:(k + 1) * P]).then_inc(f["xsT_ready"], 1)

            def give(t, k):
                act.wait_ge(f["ys_psum"], t + 1)
                if not isinstance(t, int) or t >= 2:
                    act.wait_ge(f["ys_stored"][k], (t - k) * 8)
                nc.scalar.copy(ys_sb[:, k, :], psum[:, 6, 0:D]).then_inc(f["ys_ready"], 1)

            def step(t, k):
                silu(t, k)
                if not isinstance(t, int) or t + 1 < SLOT_TILES:
                    turn(t + 1, 1 - k)
                if not isinstance(t, int) or t >= 1:
                    give(t - 1, 1 - k)

            turn(0, 0)
            for t in range(4):
                step(t, t % 2)
            with act.Fori(2, (SLOT_TILES - 1) // 2) as i:
                step(2 * i, 0)
                step(2 * i + 1, 1)
            step(SLOT_TILES - 1, 0)
            give(SLOT_TILES - 1, 0)

        def ffn_tensor(pe, f):
            keep_warm(16, NG)
            norm_transposes(pe, f["norm"], 0)
            pe.wait_ge(loaded_small, 32)
            for j in range(NT):
                wait_xnT(pe, f["norm"], j // GROUP)
                nc.tensor.matmul(psum[:, 4, j * E:(j + 1) * E], xnT[:, j * P:(j + 1) * P], router_sb[:],
                                 start=True, stop=True).then_inc(f["logits_psum"], 1)
            pe.wait_ge(f["chosen_ready"], 1)
            pe.wait_ge(consts_ready, 1)
            flat = chosen[:].rearrange("p e j -> p (e j)")
            nc.tensor.matmul(psum[:, 5, 0:E * NT], earlier[:], flat, start=True, stop=True).then_inc(f["prefix_psum"], 1)
            nc.tensor.matmul(psum[:, 6, 0:E * NT], ones[:], flat, start=True, stop=True).then_inc(f["prefix_psum"], 1)
            pe.wait_ge(f["at_tile_ready"], 1)
            for j in range(NT):
                pe.wait_ge(f["at_lane_ready"], j // GROUP + 1)
                last = nc.tensor.matmul(psum[:, 7, 0:3 * SLOT_TILES], at_lane[:, j, :],
                                        at_tile[:, j, :, :].rearrange("p a t -> p (a t)"),
                                        start=(j == 0), stop=(j == NT - 1))
            last.then_inc(f["info_psum"], 1)
            keep_warm(8, 0)
            pe.wait_ge(loaded_w, 16 * 2 * E)
            pe.wait_ge(f["tile_expert_ready"], 1)

            def turn(t, k):
                pe.wait_ge(f["xs_loaded"][k], (t - k) * 8 + 16)
                if not isinstance(t, int) or t >= 2:
                    pe.wait_ge(f["xsT_ready"], t - 1)
                nc.tensor.transpose(psum[:, 7, k * P:(k + 1) * P], xs_sb[:, k, :], ident[:]).then_inc(f["xsT_psum"], 1)

            def hidden(t, k, part):
                if part == 0:
                    pe.wait_ge(f["xsT_ready"], t + 1)
                    pe.wait_ge(f["w1_ready"], t + 1)
                if not isinstance(t, int) or t >= 2:
                    pe.wait_ge(f["u_ready" if part else "gate_ready"], t - 1)
                for c in range(FC):
                    last = nc.tensor.matmul(psum[:, 2 * k + part, c * P:(c + 1) * P],
                                            w1_tile[:, k, part * F + c * P:part * F + (c + 1) * P],
                                            xsT_sb[:, k, :], start=True, stop=True)
                last.then_inc(f["h_g" if part else "h_a"], 1)

            def down(t, k):
                e = nc.tensor.value_load(tile_expert[0:1, ds(t, 1)], min_val=0, max_val=E - 1)
                pe.wait_ge(f["u_ready"], t + 1)
                if not isinstance(t, int) or t >= 1:
                    pe.wait_ge(f["ys_ready"], t)
                for c in range(FC):
                    last = nc.tensor.matmul(psum[:, 6, 0:D], u_sb[:, k, c * P:(c + 1) * P],
                                            w2_sb[:, ds(e * (FC * D) + c * D, D)], start=(c == 0), stop=(c == FC - 1))
                last.then_inc(f["ys_psum"], 1)

            def step(t, k):
                hidden(t, k, 0)
                hidden(t, k, 1)
                if not isinstance(t, int) or t + 1 < SLOT_TILES:
                    turn(t + 1, 1 - k)
                if not isinstance(t, int) or t >= 1:
                    down(t - 1, 1 - k)

            turn(0, 0)
            for t in range(2):
                step(t, t % 2)
            with pe.Fori(1, (SLOT_TILES - 1) // 2) as i:
                step(2 * i, 0)
                step(2 * i + 1, 1)
            step(SLOT_TILES - 1, 0)
            down(SLOT_TILES - 1, 0)

        with nc.Block() as block:
            @block.sync
            def _(sp):
                sp.dma_start(x_tok[:].rearrange("p (j d) -> p j d", d=D),
                             x_in.rearrange("b (j p) d -> p (b j) d", p=P)).then_inc(loaded_x, 16)
                sp.dma_start(router_sb[:], router_w).then_inc(loaded_small, 16)
                sp.dma_start(router_b_sb[:], router_b.partition_broadcast(P)).then_inc(loaded_small, 16)
                for e in range(E):
                    sp.dma_start(w1_sb[:, e * 2 * F:(e + 1) * 2 * F], w1[e]).then_inc(loaded_w, 16)
                    sp.dma_start(w2_sb[:, e * FC * D:(e + 1) * FC * D].rearrange("p (c d) -> p c d", c=FC),
                                 w2[e].rearrange("(c p) d -> p c d", p=P)).then_inc(loaded_w, 16)
                for dst, src in (
                        (W_in_sb[:], W_in), (W_dt_sb[0:R, :], W_dt), (W_dt_sb[R:R + 1, :], b_dt.unsqueeze(0)),
                        (W_out_sb[:], W_out.rearrange("(h p) d -> p h d", p=P)),
                        (W_x_sb[:, :, 0:SECOND], W_x.rearrange("(h p) r -> p h r", p=P)),
                        (W_x_sb[:, :, SECOND:P], W_x[:, R:R + 2 * S].rearrange("(h p) r -> p h r", p=P)),
                        (conv_w_sb[:], conv_w.rearrange("(h p) k -> p h k", p=P)),
                        (A_sb[:], A_log.rearrange("(h p) s -> p h s", p=P)),
                        *((t[:, h:h + 1], v[h * P:(h + 1) * P].unsqueeze(1)) for h in range(NH)
                          for t, v in ((conv_b_sb, conv_b), (D_skip_sb, D_skip))),
                        (ln_g_sb[:], ln_g.partition_broadcast(P)), (ln_b_sb[:], ln_b.partition_broadcast(P))):
                    sp.dma_start(dst, src).then_inc(loaded_m, 16)
                ffn_sync(sp, FF[0])

            @block.gpsimd
            def _(pool):
                pool_chain(pool, nc.gpsimd.memset(ident[:], 0.0))
                nc.gpsimd.affine_select(out=ident[:], in_=ident[:], compare_op=ALU.not_equal, fill=1.0, base=0,
                                        pattern=[[-1, P]], channel_multiplier=1).then_inc(ident_ready, 1)
                pool.wait_ge(ident_ready, 1)
                pool_chain(pool, nc.gpsimd.memset(ones[:], 1.0))
                pool_chain(pool, nc.gpsimd.affine_select(out=earlier[:], in_=ones[:], compare_op=ALU.is_ge,
                                                         fill=0.0, base=-1, pattern=[[1, P]],
                                                         channel_multiplier=-1))
                nc.gpsimd.iota(expert_iota_i[:], [[0, NT], [1, E]], base=0, channel_multiplier=0)
                nc.gpsimd.iota(tile_iota_i[:], [[1, SLOT_TILES]], base=0, channel_multiplier=0)
                nc.gpsimd.iota(lane_iota[:], [[1, P]], base=0, channel_multiplier=0)
                nc.gpsimd.iota(token_tile_i[:], [[1, NT]], base=0, channel_multiplier=0)
                nc.gpsimd.iota(partition_i[:], [[0, 1]], base=0, channel_multiplier=1)
                pool_chain(pool, nc.gpsimd.iota(spare_row_i[:], [[P, SLOT_TILES]], base=N, channel_multiplier=1))
                nc.gpsimd.tensor_copy(expert_iota[:], expert_iota_i[:])
                nc.gpsimd.tensor_copy(tile_iota[:], tile_iota_i[:])
                nc.gpsimd.tensor_copy(token_tile[:], token_tile_i[:])
                nc.gpsimd.tensor_copy(partition[:], partition_i[:])
                nc.gpsimd.tensor_copy(spare_row[:], spare_row_i[:])
                nc.gpsimd.memset(ones_e[:], 1.0)
                pool_chain(pool, nc.gpsimd.memset(scan_keep[:], 1.0))
                nc.gpsimd.memset(scan_keep[:, :, 0:1], 0.0).then_inc(consts_ready, 1)
                ffn_gpsimd(pool, FF[0])

            @block.vector
            def _(dve):
                dve.wait_ge(loaded_x, 16)
                ffn_vector(dve, FF[0])

            @block.scalar
            def _(act):
                ffn_scalar(act, FF[0])

            @block.tensor
            def _(pe):
                pe.wait_ge(ident_ready, 1)
                ffn_tensor(pe, FF[0])

        chunk = [slice(c * CH, (c + 1) * CH) for c in range(NC)]
        dA_bank = [psum[:, h, :] for h in range(NH)]
        C_bank = [psum[:, 2 + k, :] for k in range(2)]
        B_bank = psum[:, 4, :]
        y_bank = [psum[:, 5 + h, :] for h in range(NH)]
        y_banks = psum[:, 5:5 + NH, :]
        o_bank = psum[:, 7, :]
        POOL_GROUP = NG - 1

        def scale_rows(engine, g, done):
            rows = xn_tok[:, g * GROUP * D:(g + 1) * GROUP * D].rearrange("p (j d) -> p j d", d=D)
            engine.tensor_tensor(rows, rows, ln_g_sb[:].unsqueeze(1).broadcast_to([P, GROUP, D]),
                                 ALU.mult).then_inc(done, 1)

        def add_rows(engine, g, done):
            rows = slice(g * GROUP * D, (g + 1) * GROUP * D)
            engine.tensor_tensor(x_tok[:, rows], x_tok[:, rows], xn_tok[:, rows], ALU.add).then_inc(done, 1)

        def recurrence_gpsimd(pool):
            def step(k, c, parity):
                pool.wait_ge(M["B_ready"], k + 1)
                pool.wait_ge(M["scan_done"][NH - 1], k + 1)
                nc.gpsimd.tensor_tensor(dBx[:, parity], dtx[:, :, chunk[c]],
                                        B_sb[:, parity:parity + 1, :].broadcast_to([P, NH, CH]),
                                        ALU.mult).then_inc(M["dBx_ready"], 1)

            for c in range(NC):
                if c < 2:
                    pool.wait_ge(M["dtx_ready"], NC if c else 1)
                with pool.Fori(0, S // SLOTS) as i:
                    for q in range(SLOTS):
                        step(c * S + SLOTS * i + q, c, q % 2)
            pool.wait_ge(M["out_norm"]["xn_even"], GROUP // 2 * (POOL_GROUP + 1))
            pool.wait_ge(M["out_norm"]["xn_odd"], GROUP // 2 * (POOL_GROUP + 1))
            scale_rows(nc.gpsimd, POOL_GROUP, M["scale_ready_pool"])
            pool.wait_ge(M["scale_ready_pool"], 1)
            add_rows(nc.gpsimd, POOL_GROUP, M["x_ready_pool"])
            pool.wait_ge(M["x_ready_pool"], 1)

        def recurrence_vector(dve):
            def scans(k, s, slot):
                for h in range(NH):
                    dve.wait_ge(M["dA_ready"][h], k + 1)
                    nc.vector.tensor_tensor_scan(H[:, slot, h, :], dA_bank[h], dBx[:, slot % 2, h, :],
                                                 carry[:, ds(s * NH + h, 1)],
                                                 ALU.mult, ALU.add).then_inc(M["scan_done"][h], 1)

            def product(k, slot):
                dve.wait_ge(M["C_psum"], k + 1)
                nc.vector.tensor_tensor(hC[:, slot % 2], H[:, slot],
                                        C_bank[slot % 2].unsqueeze(1).broadcast_to([P, NH, CH]),
                                        ALU.mult).then_inc(M["hC_ready"], 1)

            def gate(c):
                dve.wait_ge(M["sum_done"], c + 1)
                if c >= 1:
                    dve.wait_ge(M["o_psum"], c * GROUP)
                nc.vector.tensor_tensor(yz, y_banks, silu_z[:, :, chunk[c]], ALU.mult).then_inc(M["yz_ready"], 1)

            def finish():
                dve.wait_ge(M["scan_done"][NH - 1], NC * S + 2)
                dve.wait_ge(M["C_psum"], NC * S)
                for h in range(NH):
                    nc.vector.tensor_tensor(hC[:, 1, h], H[:, SLOTS - 1, h], C_bank[1], ALU.mult
                                            ).then_inc(M["hC_ready"], 1)
                dve.wait_ge(M["o_psum"], (NC - 1) * GROUP)
                for h in range(NH):
                    dve.wait_ge(M["sum_done"], NC + h)
                    nc.vector.tensor_tensor(yz[:, h], y_bank[h], silu_z[:, h, chunk[NC - 1]], ALU.mult
                                            ).then_inc(M["yz_ready"], 1)

            for c in range(NC):
                first = c * S
                if c % CPB == 0:
                    if c >= 1:
                        dve.wait_ge(M["carry_ready"], first)
                    nc.vector.memset(carry[:], 0.0).then_inc(M["carry_clear"], 1)
                    dve.wait_ge(M["carry_clear"], c // CPB + 1)
                for s in range(SLOTS):
                    scans(first + s, s, s)
                    if first + s >= 1:
                        product(first + s - 1, (s - 1) % SLOTS)
                    if c >= 1 and s == 1:
                        gate(c - 1)
                with dve.Fori(1, S // SLOTS) as i:
                    for slot in range(SLOTS):
                        s = SLOTS * i + slot
                        scans(first + s, s, slot)
                        product(first + s - 1, (slot - 1) % SLOTS)
            finish()
            norm_vector(dve, M["out_norm"], y_tok, arrives=(M["o_ready"], 1))
            dve.wait_ge(M["x_plus_b"], 2)
            for g in range(POOL_GROUP):
                dve.wait_ge(M["out_norm"]["xn_even"], GROUP // 2 * (g + 1))
                dve.wait_ge(M["out_norm"]["xn_odd"], GROUP // 2 * (g + 1))
                scale_rows(nc.vector, g, M["scale_ready"])
            for g in range(POOL_GROUP):
                dve.wait_ge(M["scale_ready"], g + 1)
                add_rows(nc.vector, g, M["x_ready"])
            dve.wait_ge(M["x_ready"], POOL_GROUP)

        def recurrence_scalar(act):
            def spread(k, parity):
                act.wait_ge(M["B_psum"], k + 1)
                nc.scalar.copy(B_sb[:, parity, :], B_bank).then_inc(M["B_ready"], 1)

            def decay(k, c, s):
                act.wait_ge(M["dBx_ready"], k + 1)
                for h in range(NH):
                    act.wait_ge(M["scan_done"][h], k + 2)
                    nc.scalar.activation(dA_bank[h], dt[:, h, chunk[c]], ACT.Exp,
                                         scale=neg_A[:, ds(s + h * S, 1)]).then_inc(M["dA_ready"][h], 1)

            def keep(k, s, slot):
                act.wait_ge(M["scan_done"][NH - 1], k + 3)
                nc.scalar.copy(carry[:, ds(s * NH, NH)], H[:, slot, :, CH - 1]).then_inc(M["carry_ready"], 1)

            def rows_out(c):
                act.wait_ge(M["o_psum"], (c + 1) * GROUP)
                nc.scalar.copy(y_tok[:, c * GROUP * D:(c + 1) * GROUP * D], o_bank).then_inc(M["o_ready"], 1)

            spread(0, 0)
            spread(1, 1)
            act.wait_ge(M["neg_A_ready"], 1)
            act.wait_ge(M["dt_ready"], 3)
            for c in range(NC):
                if c == 1:
                    act.wait_ge(M["dt_ready"], NC)
                first = c * S
                for s in range(SLOTS):
                    decay(first + s, c, s)
                    if first + s >= 1:
                        keep(first + s - 1, (s - 1) % S, (s - 1) % SLOTS)
                    spread(first + s + 2, s % 2)
                if c >= 2:
                    rows_out(c - 2)
                with act.Fori(1, S // SLOTS) as i:
                    for slot in range(SLOTS):
                        s = SLOTS * i + slot
                        decay(first + s, c, s)
                        keep(first + s - 1, s - 1, (slot - 1) % SLOTS)
                        spread(first + s + 2, slot % 2)
            rows_out(NC - 2)
            rows_out(NC - 1)
            norm_scalar(act, M["out_norm"], y_tok)

        def recurrence_tensor(pe):
            def spread(bank, row, c, done):
                nc.tensor.matmul(bank, pick_row[:, ds(row, 1)].broadcast_to([P, P]),
                                 bc_parts[:, c * CH:(c + 1) * CH], start=True, stop=True).then_inc(done, 1)

            def step(k, parity, C_next, B_next, c=0, s=None):
                last = s == S - 1
                final = last and c == NC - 1
                if B_next is not None:
                    pe.wait_ge(M["B_ready"], k + 4)
                    spread(B_bank, B_next[1], B_next[0], M["B_psum"])
                if s == 0 and c >= 1:
                    pe.wait_ge(M["yz_ready"], c)
                pe.wait_ge(M["hC_ready"], k + 1)
                for h in range(NH):
                    if final and h:
                        pe.wait_ge(M["hC_ready"], k + 1 + h)
                    mm = nc.tensor.matmul(y_bank[h], ident[:], hC[:, parity, h, :], start=(s == 0), stop=last)
                    if final or last and h == NH - 1:
                        mm.then_inc(M["sum_done"], 1)
                if s in (2, 3):
                    nc.tensor.matmul(y_bank[s - 2], D_diag[:, s - 2, :], xc[:, s - 2, chunk[c]],
                                     start=False, stop=False)
                spread(C_bank[parity], S + C_next[1], C_next[0], M["C_psum"])

            def project(c, t):
                pe.wait_ge(M["yz_ready"], c + 1 if c < NC - 1 else c + NH)
                if c >= 1:
                    pe.wait_ge(M["o_ready"], c)
                for h in range(NH):
                    mm = nc.tensor.matmul(o_bank[:, t * D:(t + 1) * D], yz[:, h, t * P:(t + 1) * P],
                                          W_out_sb[:, h, :], start=(h == 0), stop=(h == NH - 1))
                mm.then_inc(M["o_psum"], 1)

            pe.wait_ge(M["pick_ready"], 1)
            pe.wait_ge(M["bc3_ready"], 1)
            pe.wait_ge(M["dt_ready"], 2)
            spread(B_bank, 0, 0, M["B_psum"])
            spread(C_bank[0], S, 0, M["C_psum"])
            spread(C_bank[1], S + 1, 0, M["C_psum"])
            for n in (1, 2, 3):
                pe.wait_ge(M["B_ready"], n)
                spread(B_bank, n, 0, M["B_psum"])
            pe.wait_ge(M["bc3_ready"], NC)
            pe.wait_ge(M["dt_ready"], NC)
            AHEAD = 4
            for c in range(NC):
                k = c * S
                for s in range(AHEAD):
                    step(k + s, s % 2, (c, s + 2), (c, s + 4), c, s)
                with pe.Fori(1, S // AHEAD - 1) as i:
                    for q in range(AHEAD):
                        s = AHEAD * i + q
                        step(k + s, q % 2, (c, s + 2), (c, s + 4))
                for s in range(S - AHEAD, S):
                    if c >= 1:
                        project(c - 1, s - (S - AHEAD))
                    spread_ahead = k + s + 4 < NC * S + 2
                    step(k + s, s % 2, (c + (s + 2) // S, (s + 2) % S),
                         (c + 1, s + 4 - S) if spread_ahead else None, c, s)
            for t in range(GROUP):
                project(NC - 1, t)

        with nc.Block() as block:
            def give_back(engine, namespace, c, err_ready, log_ready, count):
                engine.wait_ge(M["round_ready"], c + 1)
                namespace.tensor_tensor(dtx[:, :, chunk[c]], soft_exp[:, c], dtx[:, :, chunk[c]],
                                        ALU.subtract).then_inc(err_ready, 1)
                engine.wait_ge(M["soft_ln_ready"], c + 1)
                engine.wait_ge(err_ready, count)
                namespace.tensor_tensor(dt[:, :, chunk[c]], dt[:, :, chunk[c]], dtx[:, :, chunk[c]],
                                        ALU.add).then_inc(log_ready, 1)

            v_banks = [psum[:, 2 * ((c + 1) % NC):2 * ((c + 1) % NC) + NH, :] for c in range(NC)]

            @block.sync
            def _(sp):
                pass

            @block.gpsimd
            def _(pool):
                nc.gpsimd.memset(dt_rank[R:R + 1, :, :], 1.0).then_inc(M["pads_clear"], 1)
                pool.wait_ge(M["pads_clear"], 1)
                nc.gpsimd.memset(xc_pre[:, :, :, 0:PAD], 0.0).then_inc(M["pads_clear"], 1)
                pool.wait_ge(M["pads_clear"], 2)
                pool_chain(pool, nc.gpsimd.memset(pick_row[:], 0.0))
                for part in (FIRST, SECOND, THIRD):
                    pool_chain(pool, nc.gpsimd.affine_select(out=pick_row[:], in_=pick_row[:],
                                                             compare_op=ALU.not_equal, fill=1.0, base=-part,
                                                             pattern=[[-1, 2 * S]], channel_multiplier=1))
                pool_chain(pool, nc.gpsimd.memset(bc_parts[0:THIRD, 0:N], 0.0))
                nc.gpsimd.memset(bc_parts[:, N:N + CH], 0.0).then_inc(M["pick_ready"], 1)
                pool.wait_ge(M["pick_ready"], 1)
                pool.wait_ge(M["norm"]["xn_even"], NT // 2)
                pool.wait_ge(M["norm"]["xn_odd"], NT // 2)
                for half in range(2):
                    rows = x_tok[:, half * N // 2:(half + 1) * N // 2].rearrange("p (j d) -> p j d", d=D)
                    nc.gpsimd.tensor_tensor(rows, rows, ln_b_sb[:].unsqueeze(1).broadcast_to([P, NT // 2, D]),
                                            ALU.add).then_inc(M["x_plus_b"], 1)
                for c in range(1, NC - 1):
                    give_back(pool, nc.gpsimd, c, M["err_ready"], M["log_ready"], c)
                recurrence_gpsimd(pool)

            @block.vector
            def _(dve):
                for h in range(NH):
                    nc.vector.sem_inc(M["scan_done"][h], 2)
                dve.wait_ge(loaded_m, 16 * M_LOADS)
                norm_vector(dve, M["norm"], x_tok)
                norm_evacuate(dve, nc.vector.tensor_copy, M["norm"], NG, range(0, NG, 2), M["norm"]["xnT_even"])
                dve.wait_ge(M["pads_clear"], 2)
                for c in range(NC):
                    b, q = divmod(c, CPB)
                    for tap in range(TAPS):
                        for h in range(NH):
                            shifted = xc_pre[:, h, b, q * CH + tap:q * CH + tap + CH]
                            w = conv_w_sb[:, h, tap:tap + 1]
                            if tap == 0:
                                dve.wait_ge(M["xc_pre_ready"], NH * c + h + 1)
                                step = nc.vector.tensor_scalar(xc[:, h, chunk[c]], shifted, w, None, ALU.mult)
                            else:
                                dve.wait_ge(M["conv_step"], NH * (TAPS * c + tap - 1) + h + 1)
                                step = nc.vector.scalar_tensor_tensor(
                                    out=xc[:, h, chunk[c]], in0=shifted, scalar=w, in1=xc[:, h, chunk[c]],
                                    op0=ALU.mult, op1=ALU.add)
                            step.then_inc(M["conv_step"], 1)
                def rest(c):
                    dve.wait_ge(M["bc_full_ready"], c + 1)
                    nc.vector.tensor_tensor(bc_rest[SECOND:P, c, :], bc_rest[SECOND:P, c, :],
                                            bc_parts[SECOND:P, chunk[c]],
                                            ALU.subtract).then_inc(M["bc_rest_ready"], 1)

                def third(c):
                    dve.wait_ge(M["bc2_ready"], c + 1)
                    nc.vector.tensor_tensor(bc_parts[THIRD:FIRST, chunk[c]], bc_rest[SECOND:P, c, :],
                                            bc_parts[SECOND:P, chunk[c]], ALU.subtract).then_inc(M["bc3_ready"], 1)

                def rounded(c):
                    dve.wait_ge(M["soft_exp_ready"], c + 1)
                    nc.vector.tensor_scalar(dtx[:, :, chunk[c]], soft_exp[:, c], 1.0, -1.0, ALU.add, ALU.add
                                            ).then_inc(M["round_ready"], 1)

                def delta(c, log_ready, log_count, n):
                    dve.wait_ge(log_ready, log_count)
                    nc.vector.scalar_tensor_tensor(out=dt[:, :, chunk[c]], in0=v_banks[c], scalar=0.0,
                                                   in1=dt[:, :, chunk[c]], op0=ALU.max, op1=ALU.add
                                                   ).then_inc(M["dt_ready"], 1)
                    dve.wait_ge(M["dt_ready"], n)
                    nc.vector.tensor_tensor(dtx[:, :, chunk[c]], dt[:, :, chunk[c]], xc[:, :, chunk[c]], ALU.mult
                                            ).then_inc(M["dtx_ready"], 1)

                for h in range(NH):
                    nc.vector.tensor_scalar(D_diag[:, h, :], ident[:], D_skip_sb[:, h:h + 1], None, ALU.mult)
                LAST = NC - 1
                rest(0)
                rest(1)
                rounded(0)
                rounded(1)
                give_back(dve, nc.vector, 0, M["dve_err_ready"], M["dve_log_ready"], 1)
                rest(2)
                delta(0, M["dve_log_ready"], 1, 1)
                rest(LAST)
                third(0)
                third(1)
                rounded(2)
                delta(1, M["log_ready"], 1, 2)
                rounded(LAST)
                give_back(dve, nc.vector, LAST, M["dve_err_ready"], M["dve_log_ready"], 2)
                third(2)
                third(LAST)
                dve.wait_ge(M["A_exp"], 1)
                nc.vector.tensor_scalar(neg_A[:], A_sb[:].rearrange("p h s -> p (h s)"), -1.0, None, ALU.mult
                                        ).then_inc(M["neg_A_ready"], 1)
                delta(LAST, M["dve_log_ready"], 2, 3)
                delta(2, M["log_ready"], 2, 4)
                recurrence_vector(dve)

            @block.scalar
            def _(act):
                act.wait_ge(loaded_m, 16 * M_LOADS)
                norm_scalar(act, M["norm"], x_tok, ACT.Silu)
                norm_evacuate(act, nc.scalar.copy, M["norm"], NG, range(1, NG, 2), M["norm"]["xnT_odd"])

                def hold(c):
                    b, q = divmod(c, CPB)
                    for h in range(NH):
                        act.wait_ge(M["xc_psum"], NH * c + h + 1)
                        nc.scalar.copy(xc_pre[:, h, b, PAD + q * CH:PAD + (q + 1) * CH],
                                       psum[:, 2 * (c % 2) + h, :]).then_inc(M["xc_pre_ready"], 1)

                def silu_gate(c):
                    act.wait_ge(M["z_psum"], c + 1)
                    nc.scalar.activation(silu_z[:, :, chunk[c]], psum[:, NG + 2 * (c % 2):NG + 2 * (c % 2) + NH, :],
                                         ACT.Silu).then_inc(M["silu_z_ready"], 1)

                def silu_conv(c):
                    for h in range(NH):
                        act.wait_ge(M["conv_step"], NH * (TAPS * c + TAPS - 1) + h + 1)
                        nc.scalar.activation(xc[:, h, chunk[c]], xc[:, h, chunk[c]], ACT.Silu,
                                             bias=conv_b_sb[:, h:h + 1]).then_inc(M["xc_ready"], 1)

                def ranks(c):
                    act.wait_ge(M["proj_psum"], c + 1)
                    if c >= 2:
                        act.wait_ge(M["v_psum"], c - 1)
                    nc.scalar.copy(dt_rank[0:R, c % 2, :], psum[0:R, c % 2, :]).then_inc(M["dtr_ready"], 1)
                    nc.scalar.copy(bc_parts[FIRST:P, chunk[c]], psum[FIRST:P, c % 2, :]).then_inc(M["bc1_ready"], 1)
                    nc.scalar.copy(bc_rest[SECOND:P, c, :], psum[SECOND:P, c % 2, :]).then_inc(M["bc_full_ready"], 1)

                def second(c):
                    act.wait_ge(M["bc_rest_ready"], c + 1)
                    nc.scalar.copy(bc_parts[SECOND:P, chunk[c]], bc_rest[SECOND:P, c, :]).then_inc(M["bc2_ready"], 1)

                def magnitude(c):
                    act.wait_ge(M["v_psum"], c + 1)
                    nc.scalar.activation(soft_exp[:, c], v_banks[c], ACT.Abs).then_inc(M["soft_abs_ready"], 1)

                def exponential(c):
                    act.wait_ge(M["soft_abs_ready"], c + 1)
                    nc.scalar.activation(soft_exp[:, c], soft_exp[:, c], ACT.Exp, scale=-1.0
                                         ).then_inc(M["soft_exp_ready"], 1)

                def logarithm(c):
                    act.wait_ge(M["soft_exp_ready"], c + 1)
                    nc.scalar.activation(dt[:, :, chunk[c]], soft_exp[:, c], ACT.Ln, bias=1.0
                                         ).then_inc(M["soft_ln_ready"], 1)

                hold(0)
                hold(1)
                silu_gate(0)
                hold(2)
                silu_gate(1)
                silu_conv(0)
                silu_conv(1)
                hold(3)
                silu_gate(2)
                ranks(0)
                silu_gate(3)
                magnitude(0)
                silu_conv(2)
                ranks(1)
                silu_conv(3)
                nc.scalar.preload_act_table_set("natural_log_exp_and_others")
                exponential(0)
                magnitude(1)
                exponential(1)
                logarithm(0)
                ranks(2)
                ranks(3)
                logarithm(1)
                second(0)
                second(1)
                magnitude(2)
                exponential(2)
                magnitude(3)
                logarithm(2)
                exponential(3)
                logarithm(3)
                nc.scalar.activation(A_sb[:], A_sb[:], ACT.Exp).then_inc(M["A_exp"], 1)
                second(2)
                second(3)
                recurrence_scalar(act)

            @block.tensor
            def _(pe):
                pe.wait_ge(loaded_m, 16 * M_LOADS)
                keep_warm(16, 0)
                norm_transposes(pe, M["norm"], NG)

                def inner(c, z):
                    wait_xnT(pe, M["norm"], c)
                    if z:
                        wait_xnT(pe, M["norm"], NG // 2 + 1)
                        wait_xnT(pe, M["norm"], NG // 2)
                    if c >= 2:
                        pe.wait_ge(M["silu_z_ready"] if z else M["xc_pre_ready"], (c - 1) * (1 if z else NH))
                    for h in range(NH):
                        m = z * NH + h
                        mm = nc.tensor.matmul(psum[:, z * NG + 2 * (c % 2) + h, :], W_in_sb[:, m * P:(m + 1) * P],
                                              xnT[:, chunk[c]], start=True, stop=True)
                        if not z:
                            mm.then_inc(M["xc_psum"], 1)
                    if z:
                        mm.then_inc(M["z_psum"], 1)

                inner(0, 0)
                inner(1, 0)
                for c in range(NC):
                    inner(c, 1)
                    if c + 2 < NC:
                        inner(c + 2, 0)

                def project(c):
                    pe.wait_ge(M["xc_ready"], NH * (c + 1))
                    if c < 2:
                        pe.wait_ge(M["xc_pre_ready"], NH * (3 + c))
                    else:
                        pe.wait_ge(M["bc_full_ready"], c - 1)
                    for h in range(NH):
                        mm = nc.tensor.matmul(psum[:, c % 2, :], W_x_sb[:, h, :], xc[:, h, chunk[c]],
                                              start=(h == 0), stop=(h == NH - 1))
                    mm.then_inc(M["proj_psum"], 1)

                def delta(c):
                    pe.wait_ge(M["dtr_ready"], c + 1)
                    pe.wait_ge(M["pads_clear"], 1)
                    if c == 0:
                        pe.wait_ge(M["xc_pre_ready"], NH * NC)
                    elif c < NC - 1:
                        pe.wait_ge(M["silu_z_ready"], c + 2)
                    else:
                        pe.wait_ge(M["bc_full_ready"], NC)
                    for h in range(NH):
                        mm = nc.tensor.matmul(v_banks[c][:, h, :], W_dt_sb[:, h * P:(h + 1) * P],
                                              dt_rank[:, c % 2, :], start=True, stop=True)
                    mm.then_inc(M["v_psum"], 1)

                project(0)
                delta(0)
                project(1)
                delta(1)
                project(2)
                project(3)
                delta(2)
                delta(3)
                recurrence_tensor(pe)

        with nc.Block() as block:
            @block.sync
            def _(sp):
                ffn_sync(sp, FF[1])
                rows = out.rearrange("b l d -> (b l) d")
                for g in range(NG):
                    sp.wait_ge(FF[1]["combined"], GROUP * (g + 1))
                    sp.dma_start(rows[g * CH:(g + 1) * CH, :].rearrange("(j p) d -> p j d", p=P),
                                 x_tok[:, g * GROUP * D:(g + 1) * GROUP * D].rearrange("p (j d) -> p j d", d=D)
                                 ).then_inc(out_stored, 16)
                sp.wait_ge(out_stored, 16 * NG)

            @block.gpsimd
            def _(pool):
                ffn_gpsimd(pool, FF[1])

            @block.vector
            def _(dve):
                ffn_vector(dve, FF[1])

            @block.scalar
            def _(act):
                ffn_scalar(act, FF[1])

            @block.tensor
            def _(pe):
                ffn_tensor(pe, FF[1])


_NAMES = ["attn_x", "attn_W_in", "attn_conv_w", "attn_conv_b", "attn_W_x", "attn_W_dt", "attn_b_dt", "attn_A_log",
          "attn_D_skip", "attn_W_out", "attn_ln_g", "attn_ln_b", "ffn_router_w", "ffn_router_b", "ffn_w1", "ffn_w2"]


def kernel(**inputs):
    import numpy as np
    import concourse.bacc as bacc
    from concourse.bass_utils import run_bass_kernel_spmd

    nc = bacc.Bacc("TRN2", target_bir_lowering=False, num_devices=1)
    arrays, args = {}, []
    for name in _NAMES:
        a = np.ascontiguousarray(inputs["L0_" + name])
        arrays[name] = a
        args.append(nc.dram_tensor(name, a.shape, mybir.dt.from_np(a.dtype), kind="ExternalInput").ap())
    shape = inputs["L0_attn_x"].shape
    args.append(nc.dram_tensor("out", shape, F32, kind="ExternalOutput").ap())
    macaron_kernel(nc, *args)
    r = run_bass_kernel_spmd(nc, [arrays], core_ids=[0])
    return r.results[0]["out"]
```
